# Optimizing a Trainium2 kernel written in Bass

```python
import numpy as np
import jax
import jax.numpy as jnp

def _softmax(x, axis=-1):
    return jax.nn.softmax(x, axis=axis)

def _gelu(x):
    return jax.nn.gelu(x, approximate=True)

def _silu(x):
    return jax.nn.silu(x)

def _sigmoid(x):
    return jax.nn.sigmoid(x)

def _layernorm(x, axis=-1, eps=1e-05):
    m = jnp.mean(x, axis=axis, keepdims=True)
    v = jnp.var(x, axis=axis, keepdims=True)
    return (x - m) / jnp.sqrt(v + eps)

def _scatter_add(tgt, idx, src, axis=0):
    return tgt.at[idx].add(src)

def _segment_sum(src, seg, n):
    return jax.ops.segment_sum(src, seg, n)
kernel_name = 'mk_gnn_resnorm_d4_gnn_r8_531321'

def setup_inputs(seed: int=0):
    np.random.seed(seed)
    _w = jnp.asarray

    def _rec_inputs():
        import jax
        import jax.numpy as jnp
        _gk = jax.random.key(seed)
        x = -0.000202 + 1 * jax.random.normal(jax.random.fold_in(_gk, 1), (6250, 128), jnp.float32)
        src = jax.random.randint(jax.random.fold_in(_gk, 2), (100000,), 0, 6250, jnp.int32)
        dst = jax.random.randint(jax.random.fold_in(_gk, 3), (100000,), 0, 6250, jnp.int32)
        _o = jnp.argsort(dst, stable=True)
        src = src[_o]
        dst = dst[_o]
        edge_weight = jax.random.uniform(jax.random.fold_in(_gk, 13), (100000,), jnp.float32, 0.0, 1)
        return (x, src, dst, edge_weight)
    x, src, dst, edge_weight = _rec_inputs()

    def _L0_gnn_setup():
        import jax, jax.numpy as jnp
        import numpy as np
        N = 6250
        E = 100000
        D = 128
        H = 256
        L = 4

        def _ln(x, g, b):
            m = jnp.mean(x, axis=-1, keepdims=True)
            v = jnp.var(x, axis=-1, keepdims=True)
            return (x - m) / jnp.sqrt(v + 1e-05) * g + b
        key = jax.random.key(seed)
        ks = jax.random.split(key, 16)

        def w(k, shape, fan):
            return jax.random.normal(k, shape, jnp.float32) / np.float32(np.sqrt(fan))
        return {'x': jax.random.normal(ks[0], (N, D), jnp.float32), 't': jax.random.uniform(ks[1], (1,), jnp.float32), 'edge_index': jax.random.randint(ks[2], (2, E), 0, N, jnp.int32), 'time_w1': w(ks[3], (1, H), 1), 'time_b1': jnp.zeros((H,), jnp.float32), 'time_w2': w(ks[4], (H, H), H), 'time_b2': jnp.zeros((H,), jnp.float32), 'in_w': w(ks[5], (D, H), D), 'in_b': jnp.zeros((H,), jnp.float32), 'gcn_w': w(ks[6], (L, H, H), H), 'gcn_b': jnp.zeros((L, H), jnp.float32), 'res_w1': w(ks[7], (L, H, H), H), 'res_b1': jnp.zeros((L, H), jnp.float32), 'res_g1': jnp.ones((L, H), jnp.float32), 'res_be1': jnp.zeros((L, H), jnp.float32), 'res_w2': w(ks[8], (L, H, H), H), 'res_b2': jnp.zeros((L, H), jnp.float32), 'res_g2': jnp.ones((L, H), jnp.float32), 'res_be2': jnp.zeros((L, H), jnp.float32), 'out_w1': w(ks[9], (H, H), H), 'out_b1': jnp.zeros((H,), jnp.float32), 'out_w2': w(ks[10], (H, D), H), 'out_b2': jnp.zeros((D,), jnp.float32)}
    _L0_gnn_all = _L0_gnn_setup()
    _L0_gnn_in = {k: v for k, v in _L0_gnn_all.items() if k in ('t', 'time_w1', 'time_b1', 'time_w2', 'time_b2', 'in_w', 'in_b', 'gcn_w', 'gcn_b', 'res_w1', 'res_b1', 'res_g1', 'res_be1', 'res_w2', 'res_b2', 'res_g2', 'res_be2', 'out_w1', 'out_b1', 'out_w2', 'out_b2')}
    del _L0_gnn_all

    def _L1_gnn_setup():
        import jax, jax.numpy as jnp
        import numpy as np
        N_NODES = 12500
        N_EDGES = 200000
        D_IN = 128
        D_OUT = 128
        key = jax.random.key(seed)
        k1, k2, k3, k4, k5, k6 = jax.random.split(key, 6)
        x = jax.random.normal(k1, (N_NODES, D_IN), dtype=jnp.float32)
        scale = 1.0 / np.sqrt(D_IN)
        W = jax.random.normal(k2, (D_IN, D_OUT), dtype=jnp.float32) * scale
        b = jax.random.normal(k3, (D_OUT,), dtype=jnp.float32) * scale
        edge_val = jax.random.uniform(k4, (N_EDGES,), dtype=jnp.float32)
        edge_row = jax.random.randint(k5, (N_EDGES,), 0, N_NODES, dtype=jnp.int64)
        edge_col = jax.random.randint(k6, (N_EDGES,), 0, N_NODES, dtype=jnp.int64)
        return {'x': x, 'W': W, 'b': b, 'edge_val': edge_val, 'edge_row': edge_row, 'edge_col': edge_col}
    _L1_gnn_all = _L1_gnn_setup()
    _L1_gnn_in = {k: v for k, v in _L1_gnn_all.items() if k in ('W', 'b')}
    del _L1_gnn_all

    def _L2_gnn_setup():
        import jax, jax.numpy as jnp
        import numpy as np
        N, E, D = (12500, 62500, 128)
        key = jax.random.key(seed)
        ks = jax.random.split(key, 8)
        s = 1.0 / np.sqrt(D)
        return {'node_feat': jax.random.normal(ks[0], (N, D), dtype=jnp.float32), 'edge_index': jax.random.randint(ks[1], (2, E), 0, N, dtype=jnp.int64), 'W_edge': jax.random.normal(ks[2], (2 * D, D), dtype=jnp.float32) * s, 'b_edge': jnp.zeros((D,), dtype=jnp.float32), 'W1': jax.random.normal(ks[3], (D, D), dtype=jnp.float32) * s, 'b1': jnp.zeros((D,), dtype=jnp.float32), 'W2': jax.random.normal(ks[4], (D, D), dtype=jnp.float32) * s, 'b2': jnp.zeros((D,), dtype=jnp.float32), 'eps': jnp.zeros((1,), dtype=jnp.float32)}
    _L2_gnn_all = _L2_gnn_setup()
    _L2_gnn_in = {k: v for k, v in _L2_gnn_all.items() if k in ('W_edge', 'b_edge', 'W1', 'b1', 'W2', 'b2', 'eps')}
    del _L2_gnn_all

    def _L3_gnn_setup():
        import jax, jax.numpy as jnp
        import numpy as np
        N_NODES = 12500
        N_EDGES = 400000
        N_IN = 128
        N_H = 128
        key = jax.random.key(seed)
        k_x, k_e, k_w = jax.random.split(key, 3)
        x = jax.random.normal(k_x, (N_NODES, N_IN), dtype=jnp.float32)
        edge_index = jax.random.randint(k_e, (2, N_EDGES), 0, N_NODES, dtype=jnp.int64)
        W = jax.random.normal(k_w, (N_IN, N_H), dtype=jnp.float32) * (1.0 / np.sqrt(N_IN))
        b = jnp.zeros((N_H,), dtype=jnp.float32)
        a = jnp.float32(0.25)
        return {'x': x, 'edge_index': edge_index, 'W': W, 'b': b, 'a': a}
    _L3_gnn_all = _L3_gnn_setup()
    _L3_gnn_in = {k: v for k, v in _L3_gnn_all.items() if k in ('W', 'b', 'a')}
    del _L3_gnn_all
    return {'x': x, 'src': src, 'dst': dst, 'edge_weight': edge_weight, 'L0_gnn_t': _L0_gnn_in['t'], 'L0_gnn_time_w1': _L0_gnn_in['time_w1'], 'L0_gnn_time_b1': _L0_gnn_in['time_b1'], 'L0_gnn_time_w2': _L0_gnn_in['time_w2'], 'L0_gnn_time_b2': _L0_gnn_in['time_b2'], 'L0_gnn_in_w': _L0_gnn_in['in_w'], 'L0_gnn_in_b': _L0_gnn_in['in_b'], 'L0_gnn_gcn_w': _L0_gnn_in['gcn_w'], 'L0_gnn_gcn_b': _L0_gnn_in['gcn_b'], 'L0_gnn_res_w1': _L0_gnn_in['res_w1'], 'L0_gnn_res_b1': _L0_gnn_in['res_b1'], 'L0_gnn_res_g1': _L0_gnn_in['res_g1'], 'L0_gnn_res_be1': _L0_gnn_in['res_be1'], 'L0_gnn_res_w2': _L0_gnn_in['res_w2'], 'L0_gnn_res_b2': _L0_gnn_in['res_b2'], 'L0_gnn_res_g2': _L0_gnn_in['res_g2'], 'L0_gnn_res_be2': _L0_gnn_in['res_be2'], 'L0_gnn_out_w1': _L0_gnn_in['out_w1'], 'L0_gnn_out_b1': _L0_gnn_in['out_b1'], 'L0_gnn_out_w2': _L0_gnn_in['out_w2'], 'L0_gnn_out_b2': _L0_gnn_in['out_b2'], 'L1_gnn_W': _L1_gnn_in['W'], 'L1_gnn_b': _L1_gnn_in['b'], 'L2_gnn_W_edge': _L2_gnn_in['W_edge'], 'L2_gnn_b_edge': _L2_gnn_in['b_edge'], 'L2_gnn_W1': _L2_gnn_in['W1'], 'L2_gnn_b1': _L2_gnn_in['b1'], 'L2_gnn_W2': _L2_gnn_in['W2'], 'L2_gnn_b2': _L2_gnn_in['b2'], 'L2_gnn_eps': _L2_gnn_in['eps'], 'L3_gnn_W': _L3_gnn_in['W'], 'L3_gnn_b': _L3_gnn_in['b'], 'L3_gnn_a': _L3_gnn_in['a']}

def reference(x, src, dst, edge_weight, L0_gnn_t, L0_gnn_time_w1, L0_gnn_time_b1, L0_gnn_time_w2, L0_gnn_time_b2, L0_gnn_in_w, L0_gnn_in_b, L0_gnn_gcn_w, L0_gnn_gcn_b, L0_gnn_res_w1, L0_gnn_res_b1, L0_gnn_res_g1, L0_gnn_res_be1, L0_gnn_res_w2, L0_gnn_res_b2, L0_gnn_res_g2, L0_gnn_res_be2, L0_gnn_out_w1, L0_gnn_out_b1, L0_gnn_out_w2, L0_gnn_out_b2, L1_gnn_W, L1_gnn_b, L2_gnn_W_edge, L2_gnn_b_edge, L2_gnn_W1, L2_gnn_b1, L2_gnn_W2, L2_gnn_b2, L2_gnn_eps, L3_gnn_W, L3_gnn_b, L3_gnn_a):
    import jax
    import jax.numpy as jnp

    def _L0_gnn_ref(x, t, edge_index, time_w1, time_b1, time_w2, time_b2, in_w, in_b, gcn_w, gcn_b, res_w1, res_b1, res_g1, res_be1, res_w2, res_b2, res_g2, res_be2, out_w1, out_b1, out_w2, out_b2):
        import jax, jax.numpy as jnp
        import numpy as np
        N = 6250
        E = 100000
        D = 128
        H = 256
        L = 4

        def _ln(x, g, b):
            m = jnp.mean(x, axis=-1, keepdims=True)
            v = jnp.var(x, axis=-1, keepdims=True)
            return (x - m) / jnp.sqrt(v + 1e-05) * g + b
        silu = jax.nn.silu
        te = silu(t[:, None] @ time_w1 + time_b1) @ time_w2 + time_b2
        h = x @ in_w + in_b + te
        loops = jnp.arange(N, dtype=edge_index.dtype)
        src = jnp.concatenate([edge_index[0], loops])
        dst = jnp.concatenate([edge_index[1], loops])
        deg = jax.ops.segment_sum(jnp.ones_like(dst, jnp.float32), dst, num_segments=N)
        dinv = jnp.where(deg > 0, 1.0 / jnp.sqrt(deg), 0.0)
        norm = (dinv[src] * dinv[dst])[:, None]
        for i in range(L):
            xw = h @ gcn_w[i]
            agg = jax.ops.segment_sum(xw[src] * norm, dst, num_segments=N) + gcn_b[i]
            h = h + agg
            r = silu(_ln(h @ res_w1[i] + res_b1[i], res_g1[i], res_be1[i]))
            r = _ln(r @ res_w2[i] + res_b2[i], res_g2[i], res_be2[i])
            h = h + r
        return silu(h @ out_w1 + out_b1) @ out_w2 + out_b2

    def _L1_gnn_ref(x, W, b, edge_val, edge_row, edge_col):
        import jax, jax.numpy as jnp
        import numpy as np
        N_NODES = 12500
        N_EDGES = 200000
        D_IN = 128
        D_OUT = 128
        support = x @ W + b
        gathered = support[edge_col] * edge_val[:, None]
        out = jax.ops.segment_sum(gathered, edge_row, num_segments=x.shape[0])
        return out

    def _L2_gnn_ref(node_feat, edge_index, W_edge, b_edge, W1, b1, W2, b2, eps):
        import jax, jax.numpy as jnp
        import numpy as np
        N, E, D = (12500, 62500, 128)
        n_nodes = node_feat.shape[0]
        src, dst = (edge_index[0], edge_index[1])
        h_src = node_feat[src]
        h_dst = node_feat[dst]
        edge_emb = jnp.concatenate([h_src, h_dst], axis=1)
        m = jax.nn.relu(edge_emb @ W_edge + b_edge)
        neigh = jax.ops.segment_sum(m, dst, num_segments=n_nodes)
        rst = (1.0 + eps[0]) * node_feat + neigh
        out = jax.nn.relu(rst @ W1 + b1) @ W2 + b2
        return out

    def _L3_gnn_ref(x, edge_index, W, b, a):
        import jax, jax.numpy as jnp
        import numpy as np
        N_NODES = 12500
        N_EDGES = 400000
        N_IN = 128
        N_H = 128
        n = x.shape[0]
        src, dst = (edge_index[0], edge_index[1])
        loop = jnp.arange(n, dtype=src.dtype)
        src_l = jnp.concatenate([src, loop])
        dst_l = jnp.concatenate([dst, loop])
        deg = jax.ops.segment_sum(jnp.ones_like(src_l, dtype=x.dtype), dst_l, num_segments=n)
        dinv = deg ** (-0.5)
        norm = dinv[src_l] * dinv[dst_l]
        h = x @ W
        msg = h[src_l] * norm[:, None]
        agg = jax.ops.segment_sum(msg, dst_l, num_segments=n)
        out = agg + b
        return jnp.where(out > 0, out, a * out)
    edge_index = jnp.stack([src, dst])
    x = _layernorm(x + _L0_gnn_ref(x, L0_gnn_t, edge_index, L0_gnn_time_w1, L0_gnn_time_b1, L0_gnn_time_w2, L0_gnn_time_b2, L0_gnn_in_w, L0_gnn_in_b, L0_gnn_gcn_w, L0_gnn_gcn_b, L0_gnn_res_w1, L0_gnn_res_b1, L0_gnn_res_g1, L0_gnn_res_be1, L0_gnn_res_w2, L0_gnn_res_b2, L0_gnn_res_g2, L0_gnn_res_be2, L0_gnn_out_w1, L0_gnn_out_b1, L0_gnn_out_w2, L0_gnn_out_b2), axis=-1)
    x = _layernorm(x + _L1_gnn_ref(x, L1_gnn_W, L1_gnn_b, edge_weight, src, dst), axis=-1)
    x = _layernorm(x + _L2_gnn_ref(x, edge_index, L2_gnn_W_edge, L2_gnn_b_edge, L2_gnn_W1, L2_gnn_b1, L2_gnn_W2, L2_gnn_b2, L2_gnn_eps), axis=-1)
    x = _layernorm(x + _L3_gnn_ref(x, edge_index, L3_gnn_W, L3_gnn_b, L3_gnn_a), axis=-1)
    return x

_drawn_inputs = setup_inputs


def setup_inputs(seed=0):
    import zlib

    import numpy as np

    out = dict(_drawn_inputs(seed))
    spreads = {'L0_gnn_time_b1': (0.0, 0.1),
     'L0_gnn_time_b2': (0.0, 0.1),
     'L0_gnn_in_b': (0.0, 0.1),
     'L0_gnn_gcn_b': (0.0, 0.1),
     'L0_gnn_res_b1': (0.0, 0.1),
     'L0_gnn_res_g1': (1.0, 0.2),
     'L0_gnn_res_be1': (0.0, 0.1),
     'L0_gnn_res_b2': (0.0, 0.1),
     'L0_gnn_res_g2': (1.0, 0.2),
     'L0_gnn_res_be2': (0.0, 0.1),
     'L0_gnn_out_b1': (0.0, 0.419),
     'L0_gnn_out_b2': (0.0, 0.1),
     'L2_gnn_b_edge': (0.0, 0.1),
     'L2_gnn_b1': (0.0, 0.8),
     'L2_gnn_b2': (0.0, 0.8),
     'L3_gnn_b': (0.0, 0.1)}
    factors = {'L0_gnn_time_w1': 8.0}
    for name, (base, spread) in spreads.items():
        noise = np.random.default_rng([zlib.crc32(name.encode()), seed]).standard_normal(out[name].shape)
        drawn = base * np.exp(spread * noise) if base else spread * noise
        out[name] = jnp.asarray(drawn.astype(out[name].dtype))
    for name, factor in factors.items():
        out[name] = (out[name] * factor).astype(out[name].dtype)
    return out
```

```python
from contextlib import ExitStack
from collections import namedtuple

import concourse.bass as bass
from concourse import mybir

f32, bf16, i32 = mybir.dt.float32, mybir.dt.bfloat16, mybir.dt.int32
ALU = mybir.AluOpType
ACT = mybir.ActivationFunctionType

N, E, D, H, L = 6250, 100000, 128, 256, 4
PB = 125
NB = N // PB
T = -(-E // 128)
NP = -(-(T + NB - 1) // 16) * 16
NC = -(-NP // 128)
U = 16
GR = 4
NG = NP // GR
UG = U // GR
EPS = 1e-5
FAR = 10000
NAMES = ["src", "dst", "edge_weight"]

SEMS = """loaded edges_padded consts chain_dve chain_pool keys_transposed keyrow_ready pair_tiles
pair_rows pairs_transposed pairs_ready deg_nodes deg_blocks deg_used deg_sum sqrt_in sqrt_out te_s te_ps
weights_loaded table_stored idx_ready onehot_ready onehot_raw part_ready acc_done dinv_ready
oht_ps oht_ready mixed msg_ready rstd_ready out_stored row0_ready
Z_xs Z_x Z_xtr Z_xt Z_hps Z_h Z_hall Z_htr Z_ht Z_yps Z_y
A_h A_hall A_tr A_ht A_ps A_t A_stat
B_z B_tr B_rt B_ps B_t B_stat
C_z C_q C_h C_hall C_tr C_ht C_yps C_y
M_z M_q M_h M_tr M_ht M_ups M_ut M_ops M_v M_stat
D_x D_init D_tr D_xt D_ps D_y
S_sum S_stat
R_cols R_rows R_onehot R_dup R_same R_far R_moved R_idx R_comb R_ct R_mixed R_msg acc_zeroed acc_loaded
E_x E_res E_init E_tr E_xt E_ps E_p E_q
F_r F_tr F_rt F_ups F_ut F_ops F_v F_stat
G_x G_res G_tr G_xt G_ps G_y
H_o H_n H_p H_v H_stat
I_o""".split()


def wait(e, sem, value):
    if not isinstance(value, int) or value > 0:
        e.wait_ge(sem, value)


def over_blocks(e, stages):
    most = max(lag for lag, _ in stages)
    first = (most + 3) // 2 * 2
    last = NB - NB % 2

    def step(s, odd):
        for lag, stage in stages:
            b = s - lag
            if not isinstance(s, int) or 0 <= b < NB:
                stage(b, (odd - lag) % 2)

    for s in range(first):
        step(s, s % 2)
    with e.Fori(first // 2, last // 2) as half:
        s = e.snap(half * 2)
        step(s, 0)
        step(s + 1, 1)
    for s in range(last, NB + most):
        step(s, s % 2)


def over_pairs(e, body):
    body(0, 0, 0, False)
    with e.Fori(1, NP // U - 1) as t:
        body(e.snap(t * U), e.snap(t * UG), t, False)
    body(NP - U, NG - UG, NP // U - 1, True)


def gnn(nc, a, out):
    ctx = ExitStack()
    with ctx:
        def sb(name, shape, dt=f32):
            return ctx.enter_context(nc.sbuf_tensor(name, shape, dt))

        S = namedtuple("Semaphores", SEMS)(*(ctx.enter_context(nc.semaphore(n)) for n in SEMS))
        gathered = [ctx.enter_context(nc.semaphore(f"gathered{k}")) for k in range(U)]

        src_pad = nc.dram_tensor("src_pad", (T, 128), i32, kind="Internal").ap()
        dst_pad = nc.dram_tensor("dst_pad", (T, 128), i32, kind="Internal").ap()
        w_pad = nc.dram_tensor("w_pad", (T, 128), f32, kind="Internal").ap()
        table_h = nc.dram_tensor("table_h", (N, H), f32, kind="Internal").ap()
        acc = [nc.dram_tensor(f"acc{j}", (N + 128, D), f32, kind="Internal").ap() for j in range(GR)]
        scattered = [ctx.enter_context(nc.semaphore(f"scattered{j}")) for j in range(GR)]
        table_d = nc.dram_tensor("table_d", (N, D), f32, kind="Internal").ap()

        A = sb("A", [128, NB * H])
        HR = sb("HR", [128, NB * H])
        X = sb("X", [128, NB * D])
        A2, H2 = NB * D, NB * D
        G = sb("G", [128, U * H])
        OH = sb("OH", [128, 4, GR, PB])
        idx_ring = sb("idx_ring", [128, U], i32)
        srcP = sb("srcP", [128, NP], i32)
        dlP = sb("dlP", [128, NP])
        wP = sb("wP", [128, NP])
        bpack = sb("bpack", [1, NG], i32)

        slots = sb("slots", [128, 5 * 2 * H])

        def pair_of_slots(k):
            return slots[:, k * 2 * H:(k + 1) * 2 * H].rearrange("p (r c) -> p r c", r=2)
        hs, zs, qs = (pair_of_slots(k) for k in range(3))
        hT, uT = (pair_of_slots(k).rearrange("p r (k n) -> p r k n", k=2)[:, :, :, 0:PB] for k in (3, 4))
        OHT = slots[:, 0:4 * H].rearrange("p (r j c) -> p r j c", r=2, j=GR)
        SAME = slots[:, 4 * H:8 * H].rearrange("p (r j c) -> p r j c", r=2, j=GR)
        COMB = G[:, 0:4 * GR * D].rearrange("p (r j c) -> p r j c", r=4, j=GR)
        s_col, w_col = sb("s_col", [128, 4, GR]), sb("w_col", [128, 4, GR])
        dup, far = sb("dup", [128, 2, GR]), sb("far", [128, 2, GR])
        moved = sb("moved", [128, 2, GR])
        s_idx = sb("s_idx", [128, 4, GR], i32)
        before, trash = sb("before", [128, 128]), sb("trash", [128, 1])
        products = X[:, 0:2 * GR * 128].rearrange("p (r j c) -> p r j c", r=2, j=GR)
        MSG = slots[:, 4 * H:8 * H].rearrange("p (r j c) -> p r j c", r=2, j=GR)
        stats = sb("stats", [128, NB, 6])
        ln = sb("ln", [128, 8, NB])
        rstd, nmr = ln[0:PB, 6, :], ln[0:PB, 7, :]
        dinv = sb("dinv", [128, NB])
        dsq = sb("dsq", [128, NB])

        ident = sb("ident", [128, 128])
        iota_i = sb("iota_i", [128, 128], i32)
        iota = sb("iota", [128, 128])
        thr_i = sb("thr_i", [128, NB - 1], i32)
        thr = sb("thr", [128, NB - 1])
        pcol_i = sb("pcol_i", [128, NC], i32)
        pcol = sb("pcol", [128, NC])
        dlast_i = sb("dlast_i", [128, NC], i32)
        dlast = sb("dlast", [128, NC])
        cols = sb("cols", [128, 5, NC])
        tile_i = sb("tile_i", [128, NC], i32)
        fill_i = sb("fill_i", [1, T * 128 - E], i32)
        fill_z = sb("fill_z", [1, T * 128 - E], i32)
        onepe = sb("onepe", [128, 1])

        w_in = sb("w_in", [128, H])
        w_t2 = sb("w_t2", [128, 2, H])
        w_g0 = sb("w_g0", [128, 2, H])
        w_o1 = sb("w_o1", [128, 2, H])
        w_o2 = sb("w_o2", [128, 2, D])
        w_l1 = sb("w_l1", [128, D])
        w_e = sb("w_e", [128, 2, D])
        w_f1 = sb("w_f1", [128, D])
        w_f2 = sb("w_f2", [128, D])
        w_l3 = sb("w_l3", [128, D])
        w_a = sb("w_a", [128, 2, H])
        w_b = sb("w_b", [128, 2, H])
        w_c = sb("w_c", [128, 2, H])
        r_b1, r_b2, r_g2, r_be2, r_gb = (sb(n, [128, H]) for n in ("r_b1", "r_b2", "r_g2", "r_be2", "r_gb"))
        r_gb0, r_row0, r_tb2 = sb("r_gb0", [128, H]), sb("r_row0", [128, H]), sb("r_tb2", [128, H])
        r_ob2, r_l1b, r_eb, r_fb2, r_l3b = (sb(n, [128, D]) for n in ("r_ob2", "r_l1b", "r_eb", "r_fb2", "r_l3b"))
        c_g1, c_be1, c_ob1 = sb("c_g1", [128, 2]), sb("c_be1", [128, 2]), sb("c_ob1", [128, 2])
        c_tw1, c_tb1, c_ts = sb("c_tw1", [128, 2]), sb("c_tb1", [128, 2]), sb("c_ts", [128, 2])
        c_fb1, c_t, c_eps, c_a = sb("c_fb1", [128, 1]), sb("c_t", [128, 1]), sb("c_eps", [128, 1]), sb("c_a", [128, 1])
        te_l = sb("te_l", [128, 2, PB])

        rows_si = A[:, 0:NC * 128].bitcast(i32)
        rows_di = A[:, 896:896 + NC * 128].bitcast(i32)
        rows_w = A[:, 1792:1792 + NC * 128]
        rows_s = A[:, 2688:2688 + NC * 128]
        rows_d = A[:, 3584:3584 + NC * 128]
        keyrow = A[:, 4480:4480 + NC * 128]
        junk = A[:, 5376:5376 + NC * 128]
        brow = A[:, 6272:6272 + NC * 128]
        bpack_f = A[0:1, 7168:7168 + NP]
        deg_n = HR[:, 0:1024].bitcast(bf16).rearrange("p (r g c) -> p r g c", r=2, g=8)[:, :, :, 0:PB]
        deg_b = HR[:, 1024:2048].bitcast(bf16).rearrange("p (r g c) -> p r g c", r=2, g=8)[:, :, :, 0:NB]
        assert NC * 128 == 896

        PS = ctx.enter_context(nc.psum_tensor("PS", [128, 8, 512], f32))
        PSF = PS[:, :, :].rearrange("p b c -> p (b c)")

        def part(g, d):
            return PS[0:PB, 2 * g:2 * g + 2, :].rearrange("p b c -> p (b c)")[:, 0:GR * d]\
                .rearrange("p (j c) -> p j c", j=GR)

        def node(buf, b, d, at=0):
            if isinstance(b, int):
                return buf[0:PB, at + b * d:at + (b + 1) * d]
            return buf[0:PB, bass.ds(b * d + at, d)]

        def column(buf, b):
            return buf[0:PB, b:b + 1] if isinstance(b, int) else buf[0:PB, bass.ds(b, 1)]

        def span(buf, i, n):
            return buf[:, i:i + n] if isinstance(i, int) else buf[:, bass.ds(i, n)]

        def stat(b):
            flat = stats[0:PB, :, :].rearrange("p b s -> p (b s)")
            return flat[:, 6 * b:6 * b + 6] if isinstance(b, int) else flat[:, bass.ds(b * 6, 6)]

        def rows(table, b):
            v = table.rearrange("(b j) d -> j b d", j=PB)
            return v[:, b, :] if isinstance(b, int) else v[:, bass.ds(b, 1), :]

        def block_at(e, word, j, d):
            b = nc.s_assert_within((word >> (6 * j)) & 63, 0, NB - 1,
                                   skip_runtime_bounds_check_because="VectorE wrote the numbers as at most NB - 1")
            return b * d

        PASSES = [(H, table_h, A, 0)] * L + [(D, table_d, HR, H2), (D, table_d, A, A2)]
        EDGE_MLP = L
        n_first, n_layer = 29, 10

        def ended(l):
            o = (l + 1) * NB
            return {
                "Z": [(S.Z_hall, NB), (S.Z_y, NB)],
                "A": [(S.A_hall, o), (S.A_stat, o)],
                "B": [(S.B_stat, o)],
                "C": [(S.C_hall, o), (S.C_y, o)],
                "M": [(S.M_stat, NB)], "D": [(S.D_init, NB), (S.D_y, NB)], "S": [(S.S_stat, NB)],
                "E": [(S.E_res, NB), (S.E_init, NB), (S.E_p, NB), (S.E_q, NB)],
                "F": [(S.F_stat, NB)], "G": [(S.G_res, NB), (S.G_y, NB)], "H": [(S.H_stat, NB)],
            }

        def phase_ended(e, phase, l=0):
            for sem, value in ended(l)[phase]:
                e.wait_ge(sem, value)

        def sums_ended(e, n):
            e.wait_ge(S.acc_done, (n + 1) * NP)

        NORMS = 2 * L + 4

        ctx.enter_context(nc.allow_non_contiguous_dma(reason="columns of small vectors"))
        block = ctx.enter_context(nc.Block())

        @block.sync
        def _(sp):
            def row(dst, v):
                sp.dma_start(dst[:, :], v.rearrange("(a n) -> a n", a=1).broadcast_to([128, v.shape[0]]))\
                    .then_inc(S.loaded, 16)

            def col(dst, v):
                sp.dma_start(dst[:, :], v.rearrange("(c p) -> p c", p=128)).then_inc(S.loaded, 16)

            def mat(dst, v):
                if len(dst.shape) == 3:
                    sp.dma_start(dst[:, :, :], v.rearrange("(k p) n -> p k n", p=128)).then_inc(S.loaded, 16)
                else:
                    sp.dma_start(dst[:, :], v).then_inc(S.loaded, 16)

            for pad, v in ((dst_pad, a.dst), (src_pad, a.src), (w_pad, a.edge_weight)):
                flat = pad.rearrange("t e -> (t e)")
                sp.dma_start(flat[0:E].rearrange("(k n) -> k n", k=16), v.rearrange("(k n) -> k n", k=16))\
                    .then_inc(S.edges_padded, 16)
            sp.wait_ge(S.chain_pool, 2)
            for pad, fill in ((dst_pad, fill_i[:, :]), (src_pad, fill_z[:, :]), (w_pad, fill_z[:, :].bitcast(f32))):
                flat = pad.rearrange("t e -> (t e)")
                sp.dma_start(flat[E:T * 128].rearrange("(a n) -> a n", a=1), fill).then_inc(S.edges_padded, 16)
            sp.wait_ge(S.edges_padded, 96)
            full = T // 128
            sp.dma_start(dlast_i[:, 0:full], dst_pad[0:full * 128, 127:128].rearrange("(c p) o -> p (c o)", p=128))\
                .then_inc(S.loaded, 16)
            sp.dma_start(dlast_i[0:T - full * 128, full:full + 1], dst_pad[full * 128:T, 127:128])\
                .then_inc(S.loaded, 16)
            def all_blocks(dst, v, sem):
                for p, n in ((0, 112), (112, PB - 112)):
                    sp.dma_start(dst[p:p + n, :].rearrange("j (b d) -> j b d", d=D),
                                 v.rearrange("(b j) d -> j b d", j=PB)[p:p + n, :, :]).then_inc(sem, 16)
            all_blocks(X, a.x, S.loaded)
            mat(w_in, a.L0_gnn_in_w)
            mat(w_t2, a.L0_gnn_time_w2)
            mat(w_g0, a.L0_gnn_gcn_w[0, :, :])
            mat(w_o1, a.L0_gnn_out_w1)
            mat(w_o2, a.L0_gnn_out_w2)
            mat(w_l1, a.L1_gnn_W)
            mat(w_e, a.L2_gnn_W_edge)
            mat(w_f1, a.L2_gnn_W1)
            mat(w_f2, a.L2_gnn_W2)
            mat(w_l3, a.L3_gnn_W)
            row(r_gb0, a.L0_gnn_gcn_b[0, :])
            row(r_row0, a.L0_gnn_in_b)
            row(r_tb2, a.L0_gnn_time_b2)
            row(r_ob2, a.L0_gnn_out_b2)
            row(r_l1b, a.L1_gnn_b)
            row(r_eb, a.L2_gnn_b_edge)
            row(r_fb2, a.L2_gnn_b2)
            row(r_l3b, a.L3_gnn_b)
            row(c_t, a.L0_gnn_t)
            row(c_eps, a.L2_gnn_eps)
            row(c_a, a.L3_gnn_a)
            col(c_ob1, a.L0_gnn_out_b1)
            col(c_tb1, a.L0_gnn_time_b1)
            col(c_fb1, a.L2_gnn_b1)
            sp.dma_start(c_tw1[:, :], a.L0_gnn_time_w1.rearrange("o (c p) -> p (o c)", p=128)).then_inc(S.loaded, 16)

            def layer_weights(l):
                m = min(l + 1, L - 1)
                for dst, v in ((w_a, a.L0_gnn_res_w1[l, :, :]), (w_b, a.L0_gnn_res_w2[l, :, :]),
                               (w_c, a.L0_gnn_gcn_w[m, :, :])):
                    sp.dma_start(dst[:, :, :], v.rearrange("(k p) n -> p k n", p=128)).then_inc(S.weights_loaded, 16)
                for dst, v in ((r_b1, a.L0_gnn_res_b1[l, :]), (r_b2, a.L0_gnn_res_b2[l, :]),
                               (r_g2, a.L0_gnn_res_g2[l, :]), (r_be2, a.L0_gnn_res_be2[l, :]),
                               (r_gb, a.L0_gnn_gcn_b[m, :])):
                    sp.dma_start(dst[:, :], v.rearrange("(a n) -> a n", a=1).broadcast_to([128, H]))\
                        .then_inc(S.weights_loaded, 16)
                for dst, v in ((c_g1, a.L0_gnn_res_g1[l, :]), (c_be1, a.L0_gnn_res_be1[l, :])):
                    sp.dma_start(dst[:, :], v.rearrange("(c p) -> p c", p=128)).then_inc(S.weights_loaded, 16)

            def store_table(table, ready, base, buf, d, at=0):
                def stage(b, r):
                    sp.wait_ge(ready, base + b + 1)
                    sp.dma_start(rows(table, b), node(buf, b, d, at)).then_inc(S.table_stored, 16)
                over_blocks(sp, [(0, stage)])

            layer_weights(0)
            sp.wait_ge(S.chain_pool, 4)
            for j in range(GR):
                sp.dma_start(acc[j].rearrange("n d -> (n d)").rearrange("(p c) -> p c", p=128),
                             HR[:, H2:H2 + N + 128]).then_inc(S.acc_zeroed, 16)
            store_table(table_h, S.Z_y, 0, A, H)
            for l in range(L - 1):
                sums_ended(sp, l)
                store_table(table_h, S.C_y, l * NB, A, H)
                phase_ended(sp, "C", l)
                layer_weights(l + 1)
            phase_ended(sp, "D")
            for j in range(GR):
                sp.wait_ge(scattered[j], 16 * NG)
            for j, (buf, at) in enumerate(((A, A2), (HR, 0), (HR, H2), (X, 0))):
                all_blocks(buf[:, at:at + NB * D], acc[j][0:N, :], S.acc_loaded)
            store_table(table_d, S.E_p, 0, A, D, A2)
            sums_ended(sp, L)
            store_table(table_d, S.G_y, 0, A, D, A2)

            def store_out(b, r):
                sp.wait_ge(S.I_o, b + 1)
                sp.dma_start(rows(out, b), node(A, b, D, A2)).then_inc(S.out_stored, 16)
            over_blocks(sp, [(0, store_out)])
            sp.wait_ge(S.out_stored, 16 * NB)
            sp.wait_ge(S.table_stored, 16 * NB * (L + 2))

        @block.gpsimd
        def _(pool):
            nc.gpsimd.memset(fill_i[:, :], FAR).then_inc(S.chain_pool, 1)
            nc.gpsimd.memset(fill_z[:, :], 0).then_inc(S.chain_pool, 1)
            nc.gpsimd.iota(iota_i[:, :], [[1, 128]], base=0, channel_multiplier=0).then_inc(S.consts, 1)
            nc.gpsimd.iota(thr_i[:, :], [[PB, NB - 1]], base=PB, channel_multiplier=0).then_inc(S.consts, 1)
            nc.gpsimd.iota(pcol_i[:, :], [[128, NC]], base=0, channel_multiplier=1).then_inc(S.consts, 1)
            nc.gpsimd.memset(ident[:, :], 0.0).then_inc(S.chain_pool, 1)
            nc.gpsimd.memset(HR[:, H2:H2 + N + 128], 0.0).then_inc(S.chain_pool, 1)
            pool.wait_ge(S.chain_pool, 3)
            nc.gpsimd.affine_select(out=ident[:, :], in_=ident[:, :], compare_op=ALU.not_equal, fill=1.0,
                                    base=0, pattern=[[-1, 128]], channel_multiplier=1).then_inc(S.consts, 1)

            pool.wait_ge(S.pair_tiles, 1)
            for c in range(NC):
                for rows_of, pad in ((rows_di, dst_pad), (rows_si, src_pad), (rows_w, w_pad)):
                    pool.indirect_dma_start(rows_of[:, c * 128:(c + 1) * 128], None, pad,
                                            bass.IndirectOffsetOnAxis(ap=tile_i[:, c:c + 1], axis=0),
                                            bounds_check=T - 1).then_inc(S.pair_rows, 16)

            due = pool.alloc_register("groups_used_due")

            def gathers(n):
                d, table, _, _ = PASSES[n]
                used = S.mixed if n == EDGE_MLP else S.part_ready
                base = 0 if n == EDGE_MLP else n * NG

                pool.wait_ge(S.table_stored, (n + 1) * NB * 16)

                pool.reg_mov(due, base + UG - 3)

                def body(i, q, t, last):
                    for g in range(UG):
                        if g % 2 == 0:
                            pool.wait_ge(S.idx_ready, n * (NP // 8) + t * 2 + g // 2 + 1)
                        if isinstance(q, int):
                            wait(pool, used, base + q + g - 3)
                        else:
                            pool.wait_ge(used, due)
                            pool.reg_add(due, due, 1)
                        for j in range(GR):
                            k = g * GR + j
                            pool.indirect_dma_start(G[:, k * d:(k + 1) * d], None, table,
                                                    bass.IndirectOffsetOnAxis(ap=idx_ring[:, k:k + 1], axis=0))\
                                .then_inc(gathered[k], 16)
                over_pairs(pool, body)

            pool.wait_ge(S.loaded, n_first * 16)
            pool.wait_ge(S.row0_ready, 1)
            pool.wait_ge(S.acc_zeroed, 16 * GR)

            def z_x(b, r):
                wait(pool, S.Z_xtr, b - 1)
                nc.gpsimd.tensor_copy(zs[0:PB, r, 0:D], node(X, b, D)).then_inc(S.Z_xs, 1)

            def z_h(b, r):
                pool.wait_ge(S.Z_h, b + 1)
                nc.gpsimd.tensor_tensor(node(HR, b, H), hs[0:PB, r, :], r_gb0[0:PB, :], ALU.add).then_inc(S.Z_hall, 1)
            over_blocks(pool, [(2, z_h), (0, z_x)])

            for l in range(L):
                gathers(l)
                sums_ended(pool, l)
                pool.wait_ge(S.weights_loaded, n_layer * 16 * (l + 1))

                def a_h(b, r):
                    pool.wait_ge(S.A_h, l * NB + b + 1)
                    nc.gpsimd.tensor_tensor(node(HR, b, H), hs[0:PB, r, :], r_be2[0:PB, :], ALU.add)\
                        .then_inc(S.A_hall, 1)
                over_blocks(pool, [(0, a_h)])
                if l < L - 1:
                    def c_h(b, r):
                        pool.wait_ge(S.C_h, l * NB + b + 1)
                        nc.gpsimd.tensor_tensor(node(HR, b, H), hs[0:PB, r, :], r_gb[0:PB, :], ALU.add)\
                            .then_inc(S.C_hall, 1)
                    over_blocks(pool, [(0, c_h)])

            def d_init(b, r):
                pool.wait_ge(S.D_x, b + 1)
                nc.gpsimd.tensor_copy(node(A, b, D), zs[0:PB, r, 0:D]).then_inc(S.D_init, 1)
            over_blocks(pool, [(0, d_init)])

            due_msg = pool.alloc_register("messages_due")
            due_scatter = [pool.alloc_register(f"scatters_due{j}") for j in range(GR)]
            pool.reg_mov(due_msg, UG + 1)
            for j in range(GR):
                pool.reg_mov(due_scatter[j], 16 * UG)

            def scatters(i, q, t, last):
                for g in range(UG):
                    if isinstance(q, int):
                        pool.wait_ge(S.R_msg, q + g + 1)
                        pool.wait_ge(S.R_idx, q + g + 1)
                    else:
                        pool.wait_ge(S.R_idx, q + g + 1)
                        pool.wait_ge(S.R_msg, due_msg)
                        pool.reg_add(due_msg, due_msg, 1)
                    for j in range(GR):
                        if isinstance(q, int):
                            wait(pool, scattered[j], 16 * (q + g))
                        else:
                            pool.wait_ge(scattered[j], due_scatter[j])
                            pool.reg_add(due_scatter[j], due_scatter[j], 16)
                        pool.indirect_dma_start(acc[j], bass.IndirectOffsetOnAxis(ap=s_idx[:, g, j:j + 1], axis=0),
                                                COMB[:, g, j, :], None, compute_op=ALU.add)\
                            .then_inc(scattered[j], 16)
            over_pairs(pool, scatters)
            pool.wait_ge(S.acc_loaded, 16 * 2 * GR)
            nc.gpsimd.tensor_tensor(HR[0:PB, H2:H2 + NB * D], HR[0:PB, H2:H2 + NB * D], X[0:PB, :], ALU.add)\
                .then_inc(S.S_sum, 1)

            def e_res(b, r):
                pool.wait_ge(S.E_x, b + 1)
                nc.gpsimd.tensor_tensor(node(X, b, D), zs[0:PB, r, 0:D], r_fb2[0:PB, :], ALU.add).then_inc(S.E_res, 1)
            over_blocks(pool, [(0, e_res)])
            gathers(L)
            sums_ended(pool, L)

            def f_r(b, r):
                wait(pool, S.F_tr, b - 1)
                nc.gpsimd.tensor_copy(zs[0:PB, r, 0:D], node(HR, b, D, H2)).then_inc(S.F_r, 1)
            over_blocks(pool, [(0, f_r)])

            def g_res(b, r):
                pool.wait_ge(S.G_x, b + 1)
                nc.gpsimd.tensor_copy(node(X, b, D), zs[0:PB, r, 0:D]).then_inc(S.G_res, 1)
            over_blocks(pool, [(0, g_res)])
            gathers(L + 1)

        @block.scalar
        def _(act):
            def act_fn(out_, in_, f, **k):
                return nc.scalar.activation(out_, in_, f, **k)

            def evacuate(tr, base, dst, free, done, d):
                def stage(b, r):
                    act.wait_ge(tr, base + b + 1)
                    wait(act, free, base + b - 1)
                    nc.scalar.copy(dst[:, r, 0:d // 128, :], PS[:, r, 0:d // 128 * 128]
                                   .rearrange("p (k n) -> p k n", n=128)[:, :, 0:PB]).then_inc(done, 1)
                return stage

            def scaled(ps, base, buf, at, d, done):
                def stage(b, r):
                    act.wait_ge(ps, base + b + 1)
                    act_fn(node(buf, b, d, at), PS[0:PB, 2 + r, 0:d], ACT.Copy, scale=column(dinv, b))\
                        .then_inc(done, 1)
                return stage

            def normed(buf, at, d, base, free, done, width=None):
                def stage(b, r):
                    for f in free:
                        wait(act, f, base + b - 1)
                    act_fn(zs[0:PB, r, 0:d], node(buf, b, d, at), ACT.Identity, scale=column(rstd, b),
                           bias=column(nmr, b)).then_inc(done, 1)
                return stage

            def root(k):
                act.wait_ge(S.sqrt_in, k + 2)
                act_fn(ln[0:PB, 5, :], ln[0:PB, 4, :], ACT.Sqrt).then_inc(S.sqrt_out, 1)
                act.wait_ge(S.rstd_ready, k + 1)

            def indices(n):
                used = S.mixed if n == EDGE_MLP else S.part_ready
                base = 0 if n == EDGE_MLP else n * NG

                def idx(i, q, h):
                    wait(act, used, base + q + 2 * h - 2)
                    nc.scalar.copy(idx_ring[:, 8 * h:8 * h + 8], span(srcP, i + 8 * h, 8)).then_inc(S.idx_ready, 1)
                if n == EDGE_MLP:
                    return idx

                def body(i, q, t, last):
                    for h in range(2):
                        idx(i, q, h)
                if n:
                    sums_ended(act, n - 1)
                else:
                    act.wait_ge(S.pairs_ready, 4)
                over_pairs(act, body)

            act.wait_ge(S.sqrt_in, 1)
            act_fn(dsq[0:PB, :], dsq[0:PB, :], ACT.Sqrt).then_inc(S.sqrt_out, 1)
            act.wait_ge(S.te_s, 1)
            act_fn(c_ts[:, :], c_ts[:, :], ACT.Silu).then_inc(S.te_s, 1)
            act.wait_ge(S.dinv_ready, 1)
            act.wait_ge(S.row0_ready, 1)

            def z_xt(b, r):
                act.wait_ge(S.Z_xtr, b + 1)
                wait(act, S.Z_hps, b - 1)
                nc.scalar.copy(uT[:, r, 0, :], PS[:, 4 + r, 0:PB]).then_inc(S.Z_xt, 1)
            over_blocks(act, [(8, scaled(S.Z_yps, 0, A, 0, H, S.Z_y)),
                              (6, evacuate(S.Z_htr, 0, hT, S.Z_yps, S.Z_ht, H)), (2, z_xt)])
            for l in range(L):
                base = l * NB
                indices(l)
                sums_ended(act, l)
                over_blocks(act, [(2, evacuate(S.A_tr, base, hT, S.A_ps, S.A_ht, H))])
                root(2 * l)

                def b_silu(b, r):
                    act.wait_ge(S.B_tr, base + b + 1)
                    wait(act, S.B_ps, base + b - 1)
                    for k in range(2):
                        ins = act_fn(hT[:, r, k, :], PS[:, r, k * 128:k * 128 + PB], ACT.Silu, scale=c_g1[:, k:k + 1],
                                     bias=c_be1[:, k:k + 1])
                    ins.then_inc(S.B_rt, 1)
                over_blocks(act, [(2, b_silu)])
                root(2 * l + 1)
                if l < L - 1:
                    over_blocks(act, [(6, scaled(S.C_yps, base, A, 0, H, S.C_y)),
                                      (4, evacuate(S.C_tr, base, hT, S.C_yps, S.C_ht, H))])

            def m_ut(b, r):
                act.wait_ge(S.M_ups, b + 1)
                wait(act, S.M_ops, b - 1)
                for k in range(2):
                    ins = act_fn(uT[:, r, k, :], PS[:, 6 + r, k * 128:k * 128 + PB], ACT.Silu, bias=c_ob1[:, k:k + 1])
                ins.then_inc(S.M_ut, 1)
            over_blocks(act, [(6, m_ut), (4, evacuate(S.M_tr, 0, hT, S.M_ups, S.M_ht, H))])
            root(2 * L)
            over_blocks(act, [(2, evacuate(S.D_tr, 0, hT, S.D_ps, S.D_xt, D)),
                              (0, normed(X, 0, D, 0, [S.D_tr, S.D_init], S.D_x))])
            phase_ended(act, "D")

            def r_cols(q, r):
                wait(act, S.R_same, q - 3)
                wait(act, S.R_rows, q - 3)
                wait(act, S.R_idx, q - 3)
                nc.scalar.copy(s_col[:, r, :], span(srcP, q * GR, GR)).then_inc(S.R_cols, 1)
                nc.scalar.copy(w_col[:, r, :], span(wP, q * GR, GR)).then_inc(S.R_cols, 1)

            def r_ct(q, r):
                act.wait_ge(S.R_comb, q + 1)
                wait(act, S.R_mixed, q - 1)
                nc.scalar.copy(OHT[0:PB, r, :, :], PS[0:PB, 2 + r, :].rearrange("p (j e) -> p j e", j=GR))\
                    .then_inc(S.R_ct, 1)

            def r_msg(q, r, slot):
                act.wait_ge(S.R_mixed, q + 1)
                for j in range(GR):
                    wait(act, scattered[j], 0 if isinstance(q, int) and q < 4 else 16 * (q - 3))
                nc.scalar.copy(COMB[:, slot, :, :], PS[:, 4 + r, :].rearrange("p (j c) -> p j c", j=GR))\
                    .then_inc(S.R_msg, 1)

            def r_body(i, first, t, last):
                for g in range(UG):
                    q = first + g
                    if not last or g + 1 < UG:
                        r_ct(q + 1, (g + 1) % 2)
                    if not last or g + 3 < UG:
                        r_cols(q + 3, (g + 3) % 4)
                    r_msg(q, g % 2, g)
            r_cols(0, 0)
            r_cols(1, 1)
            r_cols(2, 2)
            r_ct(0, 0)
            over_pairs(act, r_body)
            root(2 * L + 1)

            def e_p(b, r):
                act.wait_ge(S.E_ps, b + 1)
                nc.scalar.copy(node(A, b, D, A2), PS[0:PB, 2 + r, 0:D]).then_inc(S.E_p, 1)
            over_blocks(act, [(4, e_p), (2, evacuate(S.E_tr, 0, hT, S.E_ps, S.E_xt, D)),
                              (0, normed(A, 0, D, 0, [S.E_tr, S.E_res, S.E_init], S.E_x))])
            phase_ended(act, "E")
            idx = indices(L)

            def oht(g, r):
                act.wait_ge(S.oht_ps, g + 1)
                wait(act, S.mixed, g - 1)
                nc.scalar.copy(OHT[0:PB, r, :, :], PS[0:PB, 4 + r, :].rearrange("p (j e) -> p j e", j=GR))\
                    .then_inc(S.oht_ready, 1)

            def relu(g, r):
                act.wait_ge(S.mixed, g + 1)
                wait(act, S.part_ready, L * NG + g - 1)
                act_fn(MSG[:, r, :, :], PS[:, 6 + r, :].rearrange("p (j c) -> p j c", j=GR), ACT.Relu)\
                    .then_inc(S.msg_ready, 1)

            def mlp_body(i, first, t, last):
                for g in range(UG):
                    q = first + g
                    if g == 0:
                        idx(i, first, 1)
                    if g == 2 and not last:
                        idx(i + U, first + UG, 0)
                    if not last or g + 1 < UG:
                        oht(q + 1, (g + 1) % 2)
                    relu(q, g % 2)
            idx(0, 0, 0)
            oht(0, 0)
            over_pairs(act, mlp_body)
            sums_ended(act, L)

            def f_ut(b, r):
                act.wait_ge(S.F_ups, b + 1)
                wait(act, S.F_ops, b - 1)
                act_fn(uT[:, r, 0, :], PS[:, 6 + r, 0:PB], ACT.Relu, bias=c_fb1[:, 0:1]).then_inc(S.F_ut, 1)
            over_blocks(act, [(4, f_ut), (2, evacuate(S.F_tr, 0, hT, S.F_ups, S.F_rt, D))])
            root(2 * L + 2)
            over_blocks(act, [(4, scaled(S.G_ps, 0, A, A2, D, S.G_y)),
                              (2, evacuate(S.G_tr, 0, hT, S.G_ps, S.G_xt, D))])
            indices(L + 1)
            root(2 * L + 3)

            def i_o(b, r):
                act_fn(node(A, b, D, A2), node(A, b, D), ACT.Identity, scale=column(rstd, b), bias=column(nmr, b))\
                    .then_inc(S.I_o, 1)
            over_blocks(act, [(0, i_o)])

        @block.tensor
        def _(pe):
            def transposed(ready, base, src, d, free, done, bank=0):
                def stage(b, r):
                    pe.wait_ge(ready, base + b + 1)
                    wait(pe, free, base + b - 1)
                    for k in range(d // 128):
                        ins = nc.tensor.transpose(PS[:, bank + r, k * 128:k * 128 + PB],
                                                  src[0:PB, r, k * 128:(k + 1) * 128], ident[0:PB, 0:PB])
                    ins.then_inc(done, 1)
                return stage

            def product(ready, base, w, ks, d, free, done, src=None, bank=2):
                src = hT if src is None else src

                def stage(b, r):
                    pe.wait_ge(ready, base + b + 1)
                    wait(pe, free, base + b - 1)
                    for k in range(ks):
                        ins = nc.tensor.matmul(PS[0:PB, bank + r, 0:d], src[:, r, k, :], w(k),
                                               start=(k == 0), stop=(k == ks - 1))
                    ins.then_inc(done, 1)
                return stage

            def product_t(ready, base, w, ks, ms, free, done):
                def stage(b, r):
                    pe.wait_ge(ready, base + b + 1)
                    wait(pe, free, base + b - 1)
                    for m in range(ms):
                        for k in range(ks):
                            ins = nc.tensor.matmul(PS[:, 6 + r, m * 128:m * 128 + PB], w(k, m), hT[:, r, k, :],
                                                   start=(k == 0), stop=(k == ks - 1))
                    ins.then_inc(done, 1)
                return stage

            def segment_sums(n):
                d = PASSES[n][0]

                def body(i, first, t, last):
                    for g in range(UG):
                        q = n * NG + first + g
                        pe.wait_ge(S.onehot_ready, q + 1)
                        wait(pe, S.acc_done, n * NP + i + (g - 1) * GR)
                        for j in range(GR):
                            k = g * GR + j
                            pe.wait_ge(gathered[k], 16 * (n * (NP // U) + 1) + i)
                            ins = nc.tensor.matmul(part(g % 2, d)[:, j, :], OH[:, g, j, :], G[:, k * d:(k + 1) * d],
                                                   start=True, stop=True)
                        ins.then_inc(S.part_ready, 1)
                over_pairs(pe, body)

            def edge_messages():
                n = EDGE_MLP

                def turn(q, g):
                    pe.wait_ge(S.onehot_ready, n * NG + q + 1)
                    wait(pe, S.oht_ready, q - 1)
                    for j in range(GR):
                        ins = nc.tensor.transpose(PS[0:PB, 4 + g % 2, j * 128:(j + 1) * 128], OH[:, g % 4, j, :],
                                                  ident[:, :])
                    ins.then_inc(S.oht_ps, 1)

                def mix(q, g, i):
                    word = nc.tensor.value_load(span(bpack, q, 1))
                    pe.wait_ge(S.oht_ready, q + 1)
                    wait(pe, S.msg_ready, q - 1)
                    for j in range(GR):
                        k = g * GR + j
                        pe.wait_ge(gathered[k], 16 * (n * (NP // U) + 1) + i)
                        nc.tensor.matmul(PS[:, 6 + g % 2, j * D:(j + 1) * D], OHT[0:PB, g % 2, j, :],
                                         HR[0:PB, bass.ds(block_at(pe, word, j, D), D)], start=True, stop=False)
                        ins = nc.tensor.matmul(PS[:, 6 + g % 2, j * D:(j + 1) * D], ident[:, :],
                                               G[:, k * D:(k + 1) * D], start=False, stop=True)
                    ins.then_inc(S.mixed, 1)

                def add(q, g):
                    pe.wait_ge(S.msg_ready, q + 1)
                    wait(pe, S.acc_done, n * NP + q * GR - GR)
                    for j in range(GR):
                        ins = nc.tensor.matmul(part(g % 2, D)[:, j, :], OH[:, g % 4, j, :], MSG[:, g % 2, j, :],
                                               start=True, stop=True)
                    ins.then_inc(S.part_ready, 1)

                def body(i, first, t, last):
                    for g in range(UG):
                        q = first + g
                        if not last or g + 1 < UG:
                            turn(q + 1, g + 1)
                        mix(q, g, i)
                        if not isinstance(q, int) or q >= 1:
                            add(q - 1, (g - 1) % 4)
                turn(0, 0)
                over_pairs(pe, body)
                add(NG - 1, 3)

            pe.wait_ge(S.consts, 5)
            for c in range(NC):
                ins = nc.tensor.transpose(PSF[:, c * 128:(c + 1) * 128], cols[:, 0, c:c + 1].broadcast_to([128, 128]),
                                          ident[:, :])
            ins.then_inc(S.keys_transposed, 1)
            pe.wait_ge(S.keyrow_ready, 2)
            for t, v in enumerate((rows_d, rows_s, rows_w)):
                for c in range(NC):
                    nc.tensor.transpose(PSF[:, t * 896 + c * 128:t * 896 + (c + 1) * 128],
                                        v[:, c * 128:(c + 1) * 128], ident[:, :])
            for c in range(NC):
                ins = nc.tensor.transpose(PSF[:, 2688 + c * 128:2688 + (c + 1) * 128],
                                          cols[:, 2, c:c + 1].broadcast_to([128, 128]), ident[:, :])
            ins.then_inc(S.pairs_transposed, 1)
            pe.wait_ge(S.pairs_ready, 4)

            def deg_step(q, r, start, stop):
                pe.wait_ge(S.deg_nodes, q + 1)
                pe.wait_ge(S.deg_blocks, q + 1)
                for j in range(8):
                    ins = nc.tensor.matmul(PS[0:PB, 0, 0:NB], deg_n[:, r, j, :], deg_b[:, r, j, :],
                                           start=start and j == 0, stop=stop and j == 7)
                ins.then_inc(S.deg_used, 1)
            deg_step(0, 0, True, False)
            deg_step(1, 1, False, False)
            with nc.tensor.Fori(1, NP // 16 - 1) as half:
                q = nc.tensor.snap(half * 2)
                deg_step(q, 0, False, False)
                deg_step(q + 1, 1, False, False)
            deg_step(NP // 8 - 2, 0, False, False)
            deg_step(NP // 8 - 1, 1, False, True)
            pe.wait_ge(S.te_s, 3)
            for k in range(2):
                ins = nc.tensor.matmul(PS[0:PB, 1, 0:H], te_l[:, k, :], w_t2[:, k, :], start=(k == 0), stop=(k == 1))
            ins.then_inc(S.te_ps, 1)
            pe.wait_ge(S.row0_ready, 1)
            pe.wait_ge(S.dinv_ready, 1)
            over_blocks(pe, [(7, product(S.Z_ht, 0, lambda k: w_g0[:, k, :], 2, H, S.Z_y, S.Z_yps)),
                             (5, transposed(S.Z_h, 0, hs, H, S.Z_ht, S.Z_htr)),
                             (3, product(S.Z_xt, 0, lambda k: w_in[:, :], 1, H, S.Z_h, S.Z_hps, uT, 6)),
                             (1, transposed(S.Z_xs, 0, zs, D, S.Z_xt, S.Z_xtr, 4))])
            for l in range(L):
                base = l * NB
                phase_ended(pe, "Z") if l == 0 else phase_ended(pe, "C", l - 1)
                segment_sums(l)
                sums_ended(pe, l)
                pe.wait_ge(S.weights_loaded, n_layer * 16 * (l + 1))
                over_blocks(pe, [(3, product(S.A_ht, base, lambda k: w_a[:, k, :], 2, H, S.A_t, S.A_ps)),
                                 (1, transposed(S.A_h, base, hs, H, S.A_ht, S.A_tr))])
                over_blocks(pe, [(3, product(S.B_rt, base, lambda k: w_b[:, k, :], 2, H, S.B_t, S.B_ps)),
                                 (1, transposed(S.B_z, base, zs, H, S.B_rt, S.B_tr))])
                if l < L - 1:
                    over_blocks(pe, [(5, product(S.C_ht, base, lambda k: w_c[:, k, :], 2, H, S.C_y, S.C_yps)),
                                     (3, transposed(S.C_h, base, hs, H, S.C_ht, S.C_tr))])
            over_blocks(pe, [(7, product(S.M_ut, 0, lambda k: w_o2[:, k, :], 2, D, S.M_v, S.M_ops, uT, 4)),
                             (5, product_t(S.M_ht, 0, lambda k, m: w_o1[:, k, m * 128:(m + 1) * 128], 2, 2, S.M_ut,
                                           S.M_ups)),
                             (3, transposed(S.M_h, 0, hs, H, S.M_ht, S.M_tr))])
            over_blocks(pe, [(3, product(S.D_xt, 0, lambda k: w_l1[:, :], 1, D, S.D_y, S.D_ps)),
                             (1, transposed(S.D_x, 0, zs, D, S.D_xt, S.D_tr))])
            phase_ended(pe, "D")

            def r_rows(q, r, slot):
                pe.wait_ge(S.R_cols, 2 * q + 2)
                wait(pe, S.R_same, q - 1)
                for j in range(GR):
                    ins = nc.tensor.transpose(PS[:, r, j * 128:(j + 1) * 128],
                                              s_col[:, slot, j:j + 1].broadcast_to([128, 128]), ident[:, :])
                ins.then_inc(S.R_rows, 1)

            def r_comb(q, r, slot):
                pe.wait_ge(S.R_onehot, q + 1)
                pe.wait_ge(S.R_same, q + 1)
                wait(pe, S.R_ct, q - 1)
                for j in range(GR):
                    ins = nc.tensor.matmul(PS[0:PB, 2 + r, j * 128:(j + 1) * 128], OH[:, slot, j, :],
                                           SAME[:, r, j, :], start=True, stop=True)
                ins.then_inc(S.R_comb, 1)

            def r_mix(q, r):
                word = nc.tensor.value_load(span(bpack, q, 1))
                pe.wait_ge(S.R_ct, q + 1)
                wait(pe, S.R_msg, q - 1)
                for j in range(GR):
                    ins = nc.tensor.matmul(PS[:, 4 + r, j * D:(j + 1) * D], OHT[0:PB, r, j, :],
                                           HR[0:PB, bass.ds(block_at(pe, word, j, D), D)], start=True, stop=True)
                ins.then_inc(S.R_mixed, 1)

            def r_body(i, first, t, last):
                for g in range(UG):
                    q = first + g
                    if not last or g + 2 < UG:
                        r_rows(q + 2, g % 2, (g + 2) % 4)
                    if not last or g + 1 < UG:
                        r_comb(q + 1, (g + 1) % 2, (g + 1) % 4)
                    r_mix(q, g % 2)
            r_rows(0, 0, 0)
            r_rows(1, 1, 1)
            r_comb(0, 0, 0)
            over_pairs(pe, r_body)
            for j in range(GR):
                pe.wait_ge(scattered[j], 16 * NG)
            def e_product(b, r):
                pe.wait_ge(S.E_xt, b + 1)
                wait(pe, S.E_p, b - 1)
                wait(pe, S.E_q, b - 1)
                for k in range(2):
                    ins = nc.tensor.matmul(PS[0:PB, 2 + 4 * k + r, 0:D], hT[:, r, 0, :], w_e[:, k, :], start=True,
                                           stop=True)
                ins.then_inc(S.E_ps, 1)
            over_blocks(pe, [(3, e_product), (1, transposed(S.E_x, 0, zs, D, S.E_xt, S.E_tr))])
            phase_ended(pe, "E")
            edge_messages()
            sums_ended(pe, L)
            over_blocks(pe, [(5, product(S.F_ut, 0, lambda k: w_f2[:, :], 1, D, S.F_v, S.F_ops, uT, 4)),
                             (3, product_t(S.F_rt, 0, lambda k, m: w_f1[:, :], 1, 1, S.F_ut, S.F_ups)),
                             (1, transposed(S.F_r, 0, zs, D, S.F_rt, S.F_tr))])
            over_blocks(pe, [(3, product(S.G_xt, 0, lambda k: w_l3[:, :], 1, D, S.G_y, S.G_ps)),
                             (1, transposed(S.G_x, 0, zs, D, S.G_xt, S.G_tr))])
            phase_ended(pe, "G")
            segment_sums(L + 1)

        @block.vector
        def _(dve):
            chained = [0]

            def link(ins):
                chained[0] += 1
                ins.then_inc(S.chain_dve, 1)
                dve.wait_ge(S.chain_dve, chained[0])

            v = nc.vector

            def norm(k, d):
                st = stats[0:PB, :, :]
                me, se, mo, so = st[:, :, 1], st[:, :, 2], st[:, :, 4], st[:, :, 5]
                w = [ln[0:PB, q, :] for q in range(8)]
                link(v.tensor_tensor(w[0], me, mo, ALU.add))
                link(v.tensor_tensor(w[1], me, mo, ALU.subtract))
                link(v.scalar_tensor_tensor(w[2], w[1], 0.25, w[1], ALU.mult, ALU.mult))
                link(v.tensor_tensor(w[3], se, so, ALU.add))
                link(v.scalar_tensor_tensor(w[3], w[3], 1.0 / d, w[2], ALU.mult, ALU.add))
                v.tensor_scalar(w[4], w[3], EPS, None, ALU.add).then_inc(S.sqrt_in, 1)
                dve.wait_ge(S.sqrt_out, k + 2)
                link(v.reciprocal(rstd, w[5]))
                v.scalar_tensor_tensor(nmr, w[0], -0.5, rstd, ALU.mult, ALU.mult).then_inc(S.rstd_ready, 1)
                dve.wait_ge(S.rstd_ready, k + 1)

            def sums(n):
                d, _, buf, at = PASSES[n]

                def onehots(i, first, g):
                    q = first + g
                    slot = g % 4
                    wait(dve, S.part_ready, n * NG + q - 3)
                    st = i + g * GR
                    ins = v.tensor_tensor(OH[:, slot, :, :], iota[:, 0:PB].unsqueeze(1).broadcast_to([128, GR, PB]),
                                          span(dlP, st, GR).unsqueeze(2).broadcast_to([128, GR, PB]), ALU.is_equal)
                    ins.then_inc(S.onehot_ready, 1)
                onehots(0, 0, 0)
                onehots(0, 0, 1)
                onehots(0, 0, 2)
                dve.wait_ge(S.table_stored, (n + 1) * NB * 16)

                def body(i, first, t, last):
                    for g in range(UG):
                        if not last or g + 3 < UG:
                            onehots(i, first, g + 3)
                        word = v.value_load(span(bpack, first + g, 1))
                        dve.wait_ge(S.part_ready, n * NG + first + g + 1)
                        for j in range(GR):
                            off = block_at(dve, word, j, d)
                            here = buf[0:PB, bass.ds(off + at, d)]
                            wait(dve, S.acc_done, n * NP + i + g * GR + j)
                            v.tensor_tensor(here, part(g % 2, d)[:, j, :], here, ALU.add).then_inc(S.acc_done, 1)
                over_pairs(dve, body)
                sums_ended(dve, n)

            dve.wait_ge(S.loaded, n_first * 16)
            dve.wait_ge(S.consts, 4)
            link(v.tensor_copy(iota[:, :], iota_i[:, :]))
            link(v.tensor_copy(thr[:, :], thr_i[:, :]))
            link(v.tensor_copy(pcol[:, :], pcol_i[:, :]))
            link(v.memset(dlast[:, :], float(FAR)))
            full = T // 128
            link(v.tensor_copy(dlast[:, 0:full], dlast_i[:, 0:full]))
            link(v.tensor_copy(dlast[0:T - full * 128, full:full + 1], dlast_i[0:T - full * 128, full:full + 1]))
            for c in range(NC):
                link(v.tensor_scalar(junk[:, 0:NB - 1], thr[:, :], dlast[:, c:c + 1], None, ALU.is_le, ALU.add,
                                     accum_out=cols[:, 1, c:c + 1]))
            v.tensor_tensor(cols[:, 0, :], cols[:, 1, :], pcol[:, :], ALU.add).then_inc(S.consts, 1)
            dve.wait_ge(S.keys_transposed, 1)
            link(v.tensor_copy(keyrow, PSF[:, 0:NC * 128]))
            for c in range(NC):
                link(v.tensor_scalar(junk[:, 0:T], keyrow[:, 0:T], pcol[:, c:c + 1], None, ALU.is_lt, ALU.add,
                                     accum_out=cols[:, 1, c:c + 1]))
            link(v.tensor_scalar(cols[:, 1, :], cols[:, 1, :], float(T - 1), None, ALU.min))
            v.tensor_copy(tile_i[:, :], cols[:, 1, :]).then_inc(S.pair_tiles, 1)
            link(v.tensor_tensor(cols[:, 2, :], pcol[:, :], cols[:, 1, :], ALU.subtract))
            link(v.tensor_scalar(cols[:, 3, :], cols[:, 2, :], float(PB), None, ALU.mult))
            dve.wait_ge(S.pair_rows, 16 * 3 * NC)
            v.tensor_copy(rows_s, rows_si).then_inc(S.keyrow_ready, 1)
            v.tensor_tensor(rows_d.rearrange("p (c e) -> p c e", c=NC), rows_di.rearrange("p (c e) -> p c e", c=NC),
                            cols[:, 3, :].unsqueeze(2).broadcast_to([128, NC, 128]), ALU.subtract)\
                .then_inc(S.keyrow_ready, 1)
            dve.wait_ge(S.pairs_transposed, 1)
            v.tensor_copy(dlP[:, :], PSF[:, 0:NP]).then_inc(S.pairs_ready, 1)
            v.tensor_copy(srcP[:, :], PSF[:, 896:896 + NP]).then_inc(S.pairs_ready, 1)
            v.tensor_copy(wP[:, :], PSF[:, 1792:1792 + NP]).then_inc(S.pairs_ready, 1)
            v.tensor_copy(brow, PSF[:, 2688:2688 + NC * 128]).then_inc(S.pairs_ready, 1)
            dve.wait_ge(S.pairs_ready, 4)
            link(v.tensor_scalar(bpack_f, brow[0:1, 0:NP], float(NB - 1), None, ALU.min))
            four = bpack_f.rearrange("p (g j) -> p g j", j=GR)
            for j in range(GR - 1, 1, -1):
                link(v.scalar_tensor_tensor(four[:, :, j - 1], four[:, :, j], 64.0, four[:, :, j - 1], ALU.mult,
                                            ALU.add))
            v.scalar_tensor_tensor(bpack[:, :], four[:, :, 1], 64.0, four[:, :, 0], ALU.mult, ALU.add)\
                .then_inc(S.pairs_ready, 1)
            dve.wait_ge(S.pairs_ready, 5)

            def deg_step(q, r):
                wait(dve, S.deg_used, q - 1)
                v.tensor_tensor(deg_n[:, r, :, :], iota[:, 0:PB].unsqueeze(1).broadcast_to([128, 8, PB]),
                                span(dlP, q * 8, 8).unsqueeze(2).broadcast_to([128, 8, PB]), ALU.is_equal)\
                    .then_inc(S.deg_nodes, 1)
                v.tensor_tensor(deg_b[:, r, :, :], iota[:, 0:NB].unsqueeze(1).broadcast_to([128, 8, NB]),
                                span(brow, q * 8, 8).unsqueeze(2).broadcast_to([128, 8, NB]), ALU.is_equal)\
                    .then_inc(S.deg_blocks, 1)
            deg_step(0, 0)
            deg_step(1, 1)
            with nc.vector.Fori(1, NP // 16) as half:
                q = nc.vector.snap(half * 2)
                deg_step(q, 0)
                deg_step(q + 1, 1)
            dve.wait_ge(S.deg_used, NP // 8)
            v.tensor_scalar(dsq[0:PB, :], PS[0:PB, 0, 0:NB], 1.0, None, ALU.add).then_inc(S.sqrt_in, 1)
            dve.wait_ge(S.sqrt_out, 1)
            v.reciprocal(dinv[0:PB, :], dsq[0:PB, :]).then_inc(S.dinv_ready, 1)
            v.scalar_tensor_tensor(c_ts[:, :], c_tw1[:, :], c_t[:, 0:1], c_tb1[:, :], ALU.mult, ALU.add)\
                .then_inc(S.te_s, 1)
            dve.wait_ge(S.te_s, 2)
            v.tensor_copy(te_l[:, :, :], c_ts[:, :].unsqueeze(2).broadcast_to([128, 2, PB])).then_inc(S.te_s, 1)
            link(v.tensor_tensor(r_row0[:, :], r_row0[:, :], r_tb2[:, :], ALU.add))
            link(v.tensor_scalar(onepe[:, :], c_eps[:, :], 1.0, None, ALU.add))
            dve.wait_ge(S.te_ps, 1)
            v.tensor_tensor(r_row0[0:PB, :], PS[0:PB, 1, 0:H], r_row0[0:PB, :], ALU.add).then_inc(S.row0_ready, 1)
            dve.wait_ge(S.row0_ready, 1)
            dve.wait_ge(S.dinv_ready, 1)

            def z_h(b, r):
                dve.wait_ge(S.Z_hps, b + 1)
                wait(dve, S.Z_htr, b - 1)
                wait(dve, S.Z_hall, b - 1)
                v.tensor_tensor(hs[0:PB, r, :], PS[0:PB, 6 + r, 0:H], r_row0[0:PB, :], ALU.add).then_inc(S.Z_h, 1)
            over_blocks(dve, [(2, z_h)])
            dve.wait_ge(S.Z_xs, NB)
            every = X[0:PB, :].rearrange("p (b d) -> p b d", d=D)
            v.tensor_tensor(every, every, r_ob2[0:PB, :].unsqueeze(1).broadcast_to([PB, NB, D]), ALU.add)\
                .then_inc(S.Z_x, 1)
            dve.wait_ge(S.Z_x, 1)

            def biased(lag, ps, base, brow_, d, done, counted, buf=None, at=0, res=None, bank=2):
                buf = A if buf is None else buf

                def stage(b, r):
                    dve.wait_ge(ps, base + b + 1)
                    other = brow_[0:PB, :] if res is None else node(res, b, d)
                    v.tensor_tensor(node(buf, b, d, at), PS[0:PB, bank + r, 0:d], other, ALU.add).then_inc(done, 1)

                def count(b, r):
                    dve.wait_ge(done, base + b + 1)
                    v.bn_stats(stat(b), node(buf, b, d, at)).then_inc(counted, 1)
                return [(lag + 1, count), (lag, stage)]

            def normed(buf, d, base, free, done):
                def stage(b, r):
                    for f in free:
                        wait(dve, f, base + b - 1)
                    v.tensor_scalar(zs[0:PB, r, 0:d], node(buf, b, d), column(rstd, b), column(nmr, b), ALU.mult,
                                    ALU.add).then_inc(done, 1)
                return stage

            def new_h(lag, base, z, q_, h_, tr, hall):
                def gain(b, r):
                    dve.wait_ge(z, base + b + 1)
                    wait(dve, h_, base + b - 1)
                    v.tensor_tensor(qs[0:PB, r, :], zs[0:PB, r, :], r_g2[0:PB, :], ALU.mult).then_inc(q_, 1)

                def total(b, r):
                    dve.wait_ge(q_, base + b + 1)
                    wait(dve, tr, base + b - 1)
                    if hall is not None:
                        wait(dve, hall, base + b - 1)
                    v.tensor_tensor(hs[0:PB, r, :], qs[0:PB, r, :], node(HR, b, H), ALU.add).then_inc(h_, 1)
                return [(lag + 1, total), (lag, gain)]

            for l in range(L):
                base = l * NB
                sums(l)
                dve.wait_ge(S.weights_loaded, n_layer * 16 * (l + 1))

                def a_h(b, r):
                    wait(dve, S.A_tr, base + b - 1)
                    wait(dve, S.A_hall, base + b - 1)
                    v.scalar_tensor_tensor(hs[0:PB, r, :], node(A, b, H), column(dinv, b), node(HR, b, H), ALU.mult,
                                           ALU.add).then_inc(S.A_h, 1)
                over_blocks(dve, biased(4, S.A_ps, base, r_b1, H, S.A_t, S.A_stat) + [(0, a_h)])
                phase_ended(dve, "A", l)
                norm(2 * l, H)
                over_blocks(dve, biased(4, S.B_ps, base, r_b2, H, S.B_t, S.B_stat)
                            + [(0, normed(A, H, base, [S.B_tr], S.B_z))])
                phase_ended(dve, "B", l)
                norm(2 * l + 1, H)
                if l < L - 1:
                    over_blocks(dve, new_h(1, base, S.C_z, S.C_q, S.C_h, S.C_tr, S.C_hall)
                                + [(0, normed(A, H, base, [S.C_q], S.C_z))])
            over_blocks(dve, biased(8, S.M_ops, 0, None, D, S.M_v, S.M_stat, X, 0, X, 4)
                        + new_h(1, 0, S.M_z, S.M_q, S.M_h, S.M_tr, None) + [(0, normed(A, H, 0, [S.M_q], S.M_z))])
            phase_ended(dve, "M")
            norm(2 * L, D)

            def d_y(b, r):
                dve.wait_ge(S.D_ps, b + 1)
                v.tensor_tensor(node(HR, b, D), PS[0:PB, 2 + r, 0:D], r_l1b[0:PB, :], ALU.add).then_inc(S.D_y, 1)
            over_blocks(dve, [(2, d_y)])
            phase_ended(dve, "D")
            link(v.tensor_scalar(before[:, :], iota[:, :], pcol[:, 0:1], None, ALU.is_lt))
            link(v.tensor_scalar(trash[:, :], pcol[:, 0:1], float(N), None, ALU.add))

            def r_onehots(q, slot):
                wait(dve, S.R_comb, q - 3)
                v.tensor_tensor(OH[:, slot, :, :], iota[:, 0:PB].unsqueeze(1).broadcast_to([128, GR, PB]),
                                span(dlP, q * GR, GR).unsqueeze(2).broadcast_to([128, GR, PB]), ALU.is_equal)\
                    .then_inc(S.R_onehot, 1)

            def r_same(q, r, slot):
                dve.wait_ge(S.R_rows, q + 1)
                wait(dve, S.R_comb, q - 1)
                for j in range(GR):
                    row_j = PS[:, r, j * 128:(j + 1) * 128]
                    v.scalar_tensor_tensor(products[:, r, j, :], row_j, s_col[:, slot, j:j + 1], before[:, :],
                                           ALU.is_equal, ALU.mult, accum_out=dup[:, r, j:j + 1]).then_inc(S.R_dup, 1)
                    ins = v.tensor_scalar(SAME[:, r, j, :], row_j, s_col[:, slot, j:j + 1], w_col[:, slot, j:j + 1],
                                          ALU.is_equal, ALU.mult)
                ins.then_inc(S.R_same, 1)
                v.tensor_scalar(far[:, r, :], s_col[:, slot, :], -1.0, trash[:, :], ALU.mult, ALU.add)\
                    .then_inc(S.R_far, 1)

            def r_moved(q, r):
                dve.wait_ge(S.R_dup, GR * (q + 1) if isinstance(q, int) else GR * q + GR)
                dve.wait_ge(S.R_far, q + 1)
                v.scalar_tensor_tensor(moved[:, r, :], dup[:, r, :], 0.0, far[:, r, :], ALU.is_gt, ALU.mult)\
                    .then_inc(S.R_moved, 1)

            def r_idx(q, r, slot):
                dve.wait_ge(S.R_moved, q + 1)
                for j in range(GR):
                    wait(dve, scattered[j], 0 if isinstance(q, int) and q < 4 else 16 * (q - 3))
                v.tensor_tensor(s_idx[:, slot, :], moved[:, r, :], s_col[:, slot, :], ALU.add).then_inc(S.R_idx, 1)

            def r_body(i, first, t, last):
                for g in range(UG):
                    q = first + g
                    if not last or g + 2 < UG:
                        r_onehots(q + 2, (g + 2) % 4)
                    r_moved(q, g % 2)
                    if not last or g + 1 < UG:
                        r_same(q + 1, (g + 1) % 2, (g + 1) % 4)
                    r_idx(q, g % 2, g)
            r_onehots(0, 0)
            r_onehots(1, 1)
            r_same(0, 0, 0)
            over_pairs(dve, r_body)
            dve.wait_ge(S.acc_loaded, 16 * 2 * GR)
            for buf, at in ((A, A2), (HR, 0)):
                link(v.tensor_tensor(A[0:PB, 0:NB * D], A[0:PB, 0:NB * D], buf[0:PB, at:at + NB * D], ALU.add))
            dve.wait_ge(S.S_sum, 1)
            link(v.tensor_tensor(A[0:PB, 0:NB * D], A[0:PB, 0:NB * D], HR[0:PB, H2:H2 + NB * D], ALU.add))
            over_blocks(dve, [(0, lambda b, r: v.bn_stats(stat(b), node(A, b, D)).then_inc(S.S_stat, 1))])
            phase_ended(dve, "S")
            norm(2 * L + 1, D)

            def e_q(b, r):
                dve.wait_ge(S.E_ps, b + 1)
                v.tensor_tensor(node(HR, b, D), PS[0:PB, 6 + r, 0:D], r_eb[0:PB, :], ALU.add).then_inc(S.E_q, 1)

            def e_init(b, r):
                dve.wait_ge(S.E_x, b + 1)
                v.tensor_scalar(node(HR, b, D, H2), zs[0:PB, r, 0:D], onepe[0:PB, :], None, ALU.mult)\
                    .then_inc(S.E_init, 1)
            over_blocks(dve, [(4, e_q), (1, e_init)])
            phase_ended(dve, "E")
            sums(L)
            over_blocks(dve, biased(6, S.F_ops, 0, None, D, S.F_v, S.F_stat, A, 0, X, 4))
            phase_ended(dve, "F")
            norm(2 * L + 2, D)
            over_blocks(dve, [(0, normed(A, D, 0, [S.G_tr, S.G_res], S.G_x))])
            phase_ended(dve, "G")
            sums(L + 1)

            def h_o(b, r):
                wait(dve, S.H_p, b - 1)
                v.scalar_tensor_tensor(zs[0:PB, r, 0:D], node(A, b, D, A2), column(dinv, b), r_l3b[0:PB, :], ALU.mult,
                                       ALU.add).then_inc(S.H_o, 1)

            def h_n(b, r):
                dve.wait_ge(S.H_o, b + 1)
                wait(dve, S.H_p, b - 1)
                v.tensor_scalar(qs[0:PB, r, 0:D], zs[0:PB, r, 0:D], 0.0, c_a[0:PB, :], ALU.min, ALU.mult)\
                    .then_inc(S.H_n, 1)

            def h_p(b, r):
                dve.wait_ge(S.H_n, b + 1)
                wait(dve, S.H_v, b - 1)
                v.scalar_tensor_tensor(hs[0:PB, r, 0:D], zs[0:PB, r, 0:D], 0.0, qs[0:PB, r, 0:D], ALU.max, ALU.add)\
                    .then_inc(S.H_p, 1)

            def h_v(b, r):
                dve.wait_ge(S.H_p, b + 1)
                v.tensor_tensor(node(A, b, D), hs[0:PB, r, 0:D], node(X, b, D), ALU.add).then_inc(S.H_v, 1)

            def h_stat(b, r):
                dve.wait_ge(S.H_v, b + 1)
                v.bn_stats(stat(b), node(A, b, D)).then_inc(S.H_stat, 1)
            over_blocks(dve, [(4, h_stat), (3, h_v), (2, h_p), (1, h_n), (0, h_o)])
            phase_ended(dve, "H")
            norm(2 * L + 3, D)


_INS = ["x", "src", "dst", "edge_weight", "L0_gnn_t", "L0_gnn_time_w1", "L0_gnn_time_b1", "L0_gnn_time_w2",
        "L0_gnn_time_b2", "L0_gnn_in_w", "L0_gnn_in_b", "L0_gnn_gcn_w", "L0_gnn_gcn_b", "L0_gnn_res_w1",
        "L0_gnn_res_b1", "L0_gnn_res_g1", "L0_gnn_res_be1", "L0_gnn_res_w2", "L0_gnn_res_b2", "L0_gnn_res_g2",
        "L0_gnn_res_be2", "L0_gnn_out_w1", "L0_gnn_out_b1", "L0_gnn_out_w2", "L0_gnn_out_b2", "L1_gnn_W", "L1_gnn_b",
        "L2_gnn_W_edge", "L2_gnn_b_edge", "L2_gnn_W1", "L2_gnn_b1", "L2_gnn_W2", "L2_gnn_b2", "L2_gnn_eps",
        "L3_gnn_W", "L3_gnn_b", "L3_gnn_a"]


def kernel(**inputs):
    import numpy as np
    import concourse.bacc as bacc
    from concourse.bass_utils import run_bass_kernel_spmd as run

    nc = bacc.Bacc("TRN2", target_bir_lowering=False, num_devices=1)
    arrays, args = {}, {}
    for name in _INS:
        v = np.ascontiguousarray(inputs[name])
        if v.ndim == 0:
            v = v.reshape(1)
        arrays[f"in_{name}"] = v
        args[name] = nc.dram_tensor(f"in_{name}", v.shape, mybir.dt.from_np(v.dtype), kind="ExternalInput").ap()
    out = nc.dram_tensor("out_0", (N, D), f32, kind="ExternalOutput").ap()
    gnn(nc, namedtuple("Inputs", _INS)(**args), out)
    r = run(nc, [arrays], core_ids=[0])
    return r.results[0]["out_0"]
```

```python
from contextlib import ExitStack
from collections import namedtuple

import concourse.bass as bass
from concourse import mybir

f32, bf16, i32 = mybir.dt.float32, mybir.dt.bfloat16, mybir.dt.int32
ALU = mybir.AluOpType
ACT = mybir.ActivationFunctionType

N, E, D, H, L = 6250, 100000, 128, 256, 4
PB = 125
NB = N // PB
T = -(-E // 128)
NP = -(-(T + NB - 1) // 16) * 16
NC = -(-NP // 128)
U = 16
STEPS = 10
GR = 4
NG = NP // GR
UG = U // GR
EPS = 1e-5
FAR = 10000
NAMES = ["src", "dst", "edge_weight"]

SEMS = """loaded lasts_loaded edges_padded consts chain_dve chain_pool keys_transposed keyrow_ready pair_tiles
pair_rows pairs_transposed pairs_ready deg_nodes deg_used deg_counted deg_tr deg_lhs deg_sum sqrt_in sqrt_out te_s te_ps
weights_loaded table_stored idx_ready onehot_ready part_ready acc_done dinv_ready
oht_ps oht_ready mixed msg_ready rstd_ready out_stored row0_ready
Z_xs Z_x Z_yu Z_xtr Z_xt Z_hps Z_h Z_hall Z_htr Z_ht Z_yps Z_y
A_h A_hall A_tr A_ht A_ps A_t A_stat
B_z B_tr B_rt B_ps B_t B_stat
C_z C_q C_h C_hall C_tr C_ht C_yps C_y
M_z M_q M_h M_tr M_ht M_ups M_ut M_ops M_v M_stat
D_x D_init D_tr D_xt D_ps D_y
S_sum S_stat
R_cols R_rows R_onehot R_dup R_same R_far R_moved R_idx R_comb R_ct R_mixed R_msg acc_zeroed acc_loaded0 acc_loaded1
E_x E_res E_init E_tr E_xt E_ps E_p E_q
F_r F_tr F_rt F_ups F_ut F_ops F_v F_stat
G_x G_res G_tr G_xt G_ps G_y
H_o H_b H_n H_p H_v H_stat
I_m I_o""".split()


def wait(e, sem, value):
    if not isinstance(value, int) or value > 0:
        e.wait_ge(sem, value)


def over_blocks(e, stages):
    most = max(lag for lag, _ in stages)
    first = -(-(most + 2) // STEPS) * STEPS
    last = NB - NB % STEPS

    def step(s, odd):
        for lag, stage in stages:
            b = s - lag
            if not isinstance(s, int) or 0 <= b < NB:
                stage(b, (odd - lag) % 2)

    for s in range(first):
        step(s, s % 2)
    with e.Fori(first // STEPS, last // STEPS) as t:
        s = e.snap(t * STEPS)
        for k in range(STEPS):
            step(s + k, k % 2)
    for s in range(last, NB + most):
        step(s, s % 2)


def over_pairs(e, body):
    body(0, 0, 0, False)
    with e.Fori(1, NP // U - 1) as t:
        body(e.snap(t * U), e.snap(t * UG), t, False)
    body(NP - U, NG - UG, NP // U - 1, True)


def gnn(nc, a, out):
    ctx = ExitStack()
    with ctx:
        def sb(name, shape, dt=f32):
            return ctx.enter_context(nc.sbuf_tensor(name, shape, dt))

        S = namedtuple("Semaphores", SEMS)(*(ctx.enter_context(nc.semaphore(n)) for n in SEMS))
        gathered = [ctx.enter_context(nc.semaphore(f"gathered{k}")) for k in range(U)]

        src_pad = nc.dram_tensor("src_pad", (T, 128), i32, kind="Internal").ap()
        dst_pad = nc.dram_tensor("dst_pad", (T, 128), i32, kind="Internal").ap()
        w_pad = nc.dram_tensor("w_pad", (T, 128), f32, kind="Internal").ap()
        table_h = nc.dram_tensor("table_h", (N, H), f32, kind="Internal").ap()
        acc = [nc.dram_tensor(f"acc{j}", (N + 128, D), f32, kind="Internal").ap() for j in range(GR)]
        scattered = [ctx.enter_context(nc.semaphore(f"scattered{j}")) for j in range(GR)]
        table_d = nc.dram_tensor("table_d", (N, D), f32, kind="Internal").ap()

        A = sb("A", [128, NB * H])
        HR = sb("HR", [128, NB * H])
        X = sb("X", [128, NB * D])
        A2, H2 = NB * D, NB * D
        G = sb("G", [128, U * H])
        OH = sb("OH", [128, 4, GR, PB])
        idx_ring = sb("idx_ring", [128, U], i32)
        srcP = sb("srcP", [128, NP], i32)
        dlP = sb("dlP", [128, NP])
        wP = sb("wP", [128, NP])
        bpack = sb("bpack", [1, NG], i32)

        slots = sb("slots", [128, 5 * 2 * H])

        def pair_of_slots(k):
            return slots[:, k * 2 * H:(k + 1) * 2 * H].rearrange("p (r c) -> p r c", r=2)
        hs, zs, qs = (pair_of_slots(k) for k in range(3))
        hT, uT = (pair_of_slots(k).rearrange("p r (k n) -> p r k n", k=2)[:, :, :, 0:PB] for k in (3, 4))
        OHT = slots[:, 0:4 * H].rearrange("p (r j c) -> p r j c", r=2, j=GR)
        SAME = slots[:, 4 * H:8 * H].rearrange("p (r j c) -> p r j c", r=2, j=GR)
        COMB = G[:, 0:4 * GR * D].rearrange("p (r j c) -> p r j c", r=4, j=GR)
        s_col, w_col = sb("s_col", [128, 4, GR]), sb("w_col", [128, 4, GR])
        dup, far = sb("dup", [128, 2, GR]), sb("far", [128, 2, GR])
        moved = sb("moved", [128, 2, GR])
        s_idx = sb("s_idx", [128, 4, GR], i32)
        before, trash = sb("before", [128, 128]), sb("trash", [128, 1])
        products = X[:, 0:2 * GR * 128].rearrange("p (r j c) -> p r j c", r=2, j=GR)
        MSG = slots[:, 4 * H:8 * H].rearrange("p (r j c) -> p r j c", r=2, j=GR)
        stats = sb("stats", [128, NB, 6])
        ln = sb("ln", [128, 8, NB])
        rstd, nmr = ln[0:PB, 6, :], ln[0:PB, 7, :]
        dinv = sb("dinv", [128, NB])
        dsq = sb("dsq", [128, NB])

        ident = sb("ident", [128, 128])
        iota_i = sb("iota_i", [128, 128], i32)
        iota = sb("iota", [128, 128])
        thr_i = sb("thr_i", [128, NB - 1], i32)
        thr = sb("thr", [128, NB - 1])
        pcol_i = sb("pcol_i", [128, NC], i32)
        pcol = sb("pcol", [128, NC])
        dlast_i = sb("dlast_i", [128, NC], i32)
        dlast = sb("dlast", [128, NC])
        cols = sb("cols", [128, 5, NC])
        tile_i = sb("tile_i", [128, NC], i32)
        fill_i = sb("fill_i", [1, T * 128 - E], i32)
        fill_z = sb("fill_z", [1, T * 128 - E], i32)
        onepe = sb("onepe", [128, 1])
        ones = sb("ones", [128, 1], bf16)
        eps = sb("eps", [128, 1])

        w_in = sb("w_in", [128, H])
        w_t2 = sb("w_t2", [128, 2, H])
        w_g0 = sb("w_g0", [128, 2, H])
        w_o1 = sb("w_o1", [128, 2, H])
        w_o2 = sb("w_o2", [128, 2, D])
        w_l1 = sb("w_l1", [128, D])
        w_e = sb("w_e", [128, 2, D])
        w_f1 = sb("w_f1", [128, D])
        w_f2 = sb("w_f2", [128, D])
        w_l3 = sb("w_l3", [128, D])
        w_a = sb("w_a", [128, 2, H])
        w_b = sb("w_b", [128, 2, H])
        w_c = sb("w_c", [128, 2, H])
        r_b1, r_b2, r_g2, r_be2, r_gb = (sb(n, [128, H]) for n in ("r_b1", "r_b2", "r_g2", "r_be2", "r_gb"))
        r_gb0, r_row0, r_tb2 = sb("r_gb0", [128, H]), sb("r_row0", [128, H]), sb("r_tb2", [128, H])
        r_ob2, r_l1b, r_eb, r_fb2, r_l3b = (sb(n, [128, D]) for n in ("r_ob2", "r_l1b", "r_eb", "r_fb2", "r_l3b"))
        c_g1, c_be1, c_ob1 = sb("c_g1", [128, 2]), sb("c_be1", [128, 2]), sb("c_ob1", [128, 2])
        c_tw1, c_tb1, c_ts = sb("c_tw1", [128, 2]), sb("c_tb1", [128, 2]), sb("c_ts", [128, 2])
        c_fb1, c_t, c_eps, c_a = sb("c_fb1", [128, 1]), sb("c_t", [128, 1]), sb("c_eps", [128, 1]), sb("c_a", [128, 1])
        te_l = sb("te_l", [128, 2, PB])

        rows_si = A[:, 0:NC * 128].bitcast(i32)
        rows_di = A[:, 896:896 + NC * 128].bitcast(i32)
        rows_w = A[:, 1792:1792 + NC * 128]
        rows_s = A[:, 2688:2688 + NC * 128]
        rows_d = A[:, 3584:3584 + NC * 128]
        keyrow = A[:, 4480:4480 + NC * 128]
        junk = A[:, 5376:5376 + NC * 128]
        bpack_f = A[0:1, 7168:7168 + NP]
        deg_n = G[:, 0:2048].bitcast(bf16).rearrange("p (r h c g) -> p r h c g", r=2, h=2, g=8)[:, :, :, 0:PB, :]
        OHF = OH[:, :, :, :].rearrange("p r j c -> p (r j c)")
        count_t = OHF[:, 0:512].bitcast(bf16).rearrange("p (c n) -> p c n", n=128)[:, 0:NC, 0:PB]
        iota_x = OHF[:, 768:768 + 4 * PB].bitcast(bf16).rearrange("p (c g) -> p c g", g=8)
        dl16 = G[:, 2048:2048 + NP // 2].bitcast(bf16)
        pair_block = OHF[:, 512:768].bitcast(bf16).rearrange("p (c n) -> p c n", n=64)[:, 0:NC, 0:NB]
        counts = G[:, 3072:3072 + NP]
        brow = G[:, 2048:2048 + NC * 128]
        assert NC * 128 == 896

        PS = ctx.enter_context(nc.psum_tensor("PS", [128, 8, 512], f32))
        PSF = PS[:, :, :].rearrange("p b c -> p (b c)")

        def part(g, d):
            return PS[0:PB, 2 * g:2 * g + 2, :].rearrange("p b c -> p (b c)")[:, 0:GR * d]\
                .rearrange("p (j c) -> p j c", j=GR)

        def node(buf, b, d, at=0):
            if isinstance(b, int):
                return buf[0:PB, at + b * d:at + (b + 1) * d]
            return buf[0:PB, bass.ds(b * d + at, d)]

        def column(buf, b):
            return buf[0:PB, b:b + 1] if isinstance(b, int) else buf[0:PB, bass.ds(b, 1)]

        def span(buf, i, n):
            return buf[:, i:i + n] if isinstance(i, int) else buf[:, bass.ds(i, n)]

        BC = 5
        NCH = NB // BC

        def chunk(buf, c, d, at=0):
            return buf[0:PB, at + c * BC * d:at + (c + 1) * BC * d].rearrange("p (b d) -> p b d", d=d)

        def per_node(buf, c, d):
            return buf[0:PB, c * BC:(c + 1) * BC].unsqueeze(2).broadcast_to([PB, BC, d])

        def per_feature(row, d):
            return row[0:PB, :].unsqueeze(1).broadcast_to([PB, BC, d])

        def half(buf, h, at=0):
            return buf[:, at + h * (NB // 2) * D:at + (h + 1) * (NB // 2) * D]

        def stored(n):
            return 16 * (2 * NCH + n * NB)

        def stat(b):
            flat = stats[0:PB, :, :].rearrange("p b s -> p (b s)")
            return flat[:, 6 * b:6 * b + 6] if isinstance(b, int) else flat[:, bass.ds(b * 6, 6)]

        def rows(table, b):
            v = table.rearrange("(b j) d -> j b d", j=PB)
            return v[:, b, :] if isinstance(b, int) else v[:, bass.ds(b, 1), :]

        def block_at(e, word, j, d):
            b = nc.s_assert_within((word >> (6 * j)) & 63, 0, NB - 1,
                                   skip_runtime_bounds_check_because="VectorE wrote the numbers as at most NB - 1")
            return b * d

        PASSES = [(H, table_h, A, 0)] * L + [(D, table_d, HR, H2), (D, table_d, A, A2)]
        EDGE_MLP = L
        n_first, n_layer = 27, 10

        def ended(l):
            o = (l + 1) * NB
            return {
                "Z": [(S.Z_hall, NB), (S.Z_y, NCH)],
                "A": [(S.A_hall, o), (S.A_stat, o)],
                "B": [(S.B_stat, o)],
                "C": [(S.C_hall, o), (S.C_y, o)],
                "M": [(S.M_stat, NB)], "D": [(S.D_init, NB), (S.D_y, NB)], "S": [(S.S_stat, NB)],
                "E": [(S.E_res, NB), (S.E_init, NB), (S.E_p, NB), (S.E_q, NB)],
                "F": [(S.F_stat, NB)], "G": [(S.G_res, NB), (S.G_y, NB)], "H": [(S.H_stat, NB)],
            }

        def phase_ended(e, phase, l=0):
            for sem, value in ended(l)[phase]:
                e.wait_ge(sem, value)

        def sums_ended(e, n):
            e.wait_ge(S.acc_done, (n + 1) * NP)

        ctx.enter_context(nc.allow_non_contiguous_dma(reason="columns of small vectors"))
        block = ctx.enter_context(nc.Block())

        @block.sync
        def _(sp):
            def row(dst, v):
                sp.dma_start(dst[:, :], v.rearrange("(a n) -> a n", a=1).broadcast_to([128, v.shape[0]]))\
                    .then_inc(S.loaded, 16)

            def col(dst, v):
                sp.dma_start(dst[:, :], v.rearrange("(c p) -> p c", p=128)).then_inc(S.loaded, 16)

            def mat(dst, v):
                if len(dst.shape) == 3:
                    sp.dma_start(dst[:, :, :], v.rearrange("(k p) n -> p k n", p=128)).then_inc(S.loaded, 16)
                else:
                    sp.dma_start(dst[:, :], v).then_inc(S.loaded, 16)

            for pad, v in ((dst_pad, a.dst), (src_pad, a.src), (w_pad, a.edge_weight)):
                flat = pad.rearrange("t e -> (t e)")
                sp.dma_start(flat[0:E].rearrange("(k n) -> k n", k=16), v.rearrange("(k n) -> k n", k=16))\
                    .then_inc(S.edges_padded, 16)
            sp.wait_ge(S.chain_pool, 2)
            for pad, fill in ((dst_pad, fill_i[:, :]), (src_pad, fill_z[:, :]), (w_pad, fill_z[:, :].bitcast(f32))):
                flat = pad.rearrange("t e -> (t e)")
                sp.dma_start(flat[E:T * 128].rearrange("(a n) -> a n", a=1), fill).then_inc(S.edges_padded, 16)
            sp.wait_ge(S.edges_padded, 96)
            full = T // 128
            sp.dma_start(dlast_i[:, 0:full], dst_pad[0:full * 128, 127:128].rearrange("(c p) o -> p (c o)", p=128))\
                .then_inc(S.lasts_loaded, 16)
            sp.dma_start(dlast_i[0:T - full * 128, full:full + 1], dst_pad[full * 128:T, 127:128])\
                .then_inc(S.lasts_loaded, 16)

            def all_blocks(dst, v, sem):
                for p, n in ((0, 112), (112, PB - 112)):
                    sp.dma_start(dst[p:p + n, :].rearrange("j (b d) -> j b d", d=D),
                                 v.rearrange("(b j) d -> j b d", j=PB)[p:p + n, :, :]).then_inc(sem, 16)
            all_blocks(X, a.x, S.loaded)
            mat(w_in, a.L0_gnn_in_w)
            mat(w_t2, a.L0_gnn_time_w2)
            mat(w_g0, a.L0_gnn_gcn_w[0, :, :])
            mat(w_o1, a.L0_gnn_out_w1)
            mat(w_o2, a.L0_gnn_out_w2)
            mat(w_l1, a.L1_gnn_W)
            mat(w_e, a.L2_gnn_W_edge)
            mat(w_f1, a.L2_gnn_W1)
            mat(w_f2, a.L2_gnn_W2)
            mat(w_l3, a.L3_gnn_W)
            row(r_gb0, a.L0_gnn_gcn_b[0, :])
            row(r_row0, a.L0_gnn_in_b)
            row(r_tb2, a.L0_gnn_time_b2)
            row(r_ob2, a.L0_gnn_out_b2)
            row(r_l1b, a.L1_gnn_b)
            row(r_eb, a.L2_gnn_b_edge)
            row(r_fb2, a.L2_gnn_b2)
            row(r_l3b, a.L3_gnn_b)
            row(c_t, a.L0_gnn_t)
            row(c_eps, a.L2_gnn_eps)
            row(c_a, a.L3_gnn_a)
            col(c_ob1, a.L0_gnn_out_b1)
            col(c_tb1, a.L0_gnn_time_b1)
            col(c_fb1, a.L2_gnn_b1)
            sp.dma_start(c_tw1[:, :], a.L0_gnn_time_w1.rearrange("o (c p) -> p (o c)", p=128)).then_inc(S.loaded, 16)

            def layer_weights(l):
                m = min(l + 1, L - 1)
                for dst, v in ((w_a, a.L0_gnn_res_w1[l, :, :]), (w_b, a.L0_gnn_res_w2[l, :, :]),
                               (w_c, a.L0_gnn_gcn_w[m, :, :])):
                    sp.dma_start(dst[:, :, :], v.rearrange("(k p) n -> p k n", p=128)).then_inc(S.weights_loaded, 16)
                for dst, v in ((r_b1, a.L0_gnn_res_b1[l, :]), (r_b2, a.L0_gnn_res_b2[l, :]),
                               (r_g2, a.L0_gnn_res_g2[l, :]), (r_be2, a.L0_gnn_res_be2[l, :]),
                               (r_gb, a.L0_gnn_gcn_b[m, :])):
                    sp.dma_start(dst[:, :], v.rearrange("(a n) -> a n", a=1).broadcast_to([128, H]))\
                        .then_inc(S.weights_loaded, 16)
                for dst, v in ((c_g1, a.L0_gnn_res_g1[l, :]), (c_be1, a.L0_gnn_res_be1[l, :])):
                    sp.dma_start(dst[:, :], v.rearrange("(c p) -> p c", p=128)).then_inc(S.weights_loaded, 16)

            def store_table(table, ready, base, buf, d, at=0):
                def stage(b, r):
                    sp.wait_ge(ready, base + b + 1)
                    sp.dma_start(rows(table, b), node(buf, b, d, at)).then_inc(S.table_stored, 16)
                over_blocks(sp, [(0, stage)])

            layer_weights(0)
            sp.wait_ge(S.chain_pool, 4)
            for j in range(GR):
                sp.dma_start(acc[j].rearrange("n d -> (n d)").rearrange("(p c) -> p c", p=128),
                             HR[:, H2:H2 + N + 128]).then_inc(S.acc_zeroed, 16)
            for c in range(NCH):
                sp.wait_ge(S.Z_y, c + 1)
                for p, n in ((0, 112), (112, PB - 112)):
                    sp.dma_start(table_h.rearrange("(b j) d -> j b d", j=PB)[p:p + n, c * BC:(c + 1) * BC, :],
                                 chunk(A, c, H)[p:p + n, :, :]).then_inc(S.table_stored, 16)
            for l in range(L - 1):
                sums_ended(sp, l)
                store_table(table_h, S.C_y, l * NB, A, H)
                phase_ended(sp, "C", l)
                layer_weights(l + 1)
            phase_ended(sp, "D")
            for j in range(GR):
                sp.wait_ge(scattered[j], 16 * NG)
            for h, loaded in enumerate((S.acc_loaded0, S.acc_loaded1)):
                for j, (buf, at) in enumerate(((A, A2), (HR, 0), (HR, H2), (X, 0))):
                    all_blocks(half(buf, h, at), acc[j][h * N // 2:(h + 1) * N // 2, :], loaded)
            store_table(table_d, S.E_p, 0, A, D, A2)
            sums_ended(sp, L)
            store_table(table_d, S.G_y, 0, A, D, A2)

            for c in range(NCH):
                sp.wait_ge(S.I_o, c + 1)
                for p, n in ((0, 112), (112, PB - 112)):
                    sp.dma_start(out.rearrange("(b j) d -> j b d", j=PB)[p:p + n, c * BC:(c + 1) * BC, :],
                                 chunk(A, c, D, A2)[p:p + n, :, :]).then_inc(S.out_stored, 16)
            sp.wait_ge(S.out_stored, 16 * 2 * NCH)
            sp.wait_ge(S.table_stored, stored(L + 1))

        @block.gpsimd
        def _(pool):
            nc.gpsimd.memset(fill_i[:, :], FAR).then_inc(S.chain_pool, 1)
            nc.gpsimd.memset(fill_z[:, :], 0).then_inc(S.chain_pool, 1)
            nc.gpsimd.iota(iota_i[:, :], [[1, 128]], base=0, channel_multiplier=0).then_inc(S.consts, 1)
            nc.gpsimd.iota(thr_i[:, :], [[PB, NB - 1]], base=PB, channel_multiplier=0).then_inc(S.consts, 1)
            nc.gpsimd.iota(pcol_i[:, :], [[128, NC]], base=0, channel_multiplier=1).then_inc(S.consts, 1)
            nc.gpsimd.memset(ident[:, :], 0.0).then_inc(S.chain_pool, 1)
            nc.gpsimd.memset(HR[:, H2:H2 + N + 128], 0.0).then_inc(S.chain_pool, 1)
            pool.wait_ge(S.chain_pool, 3)
            nc.gpsimd.affine_select(out=ident[:, :], in_=ident[:, :], compare_op=ALU.not_equal, fill=1.0,
                                    base=0, pattern=[[-1, 128]], channel_multiplier=1).then_inc(S.consts, 1)

            pool.wait_ge(S.pair_tiles, 1)
            for c in range(NC):
                for rows_of, pad in ((rows_di, dst_pad), (rows_si, src_pad), (rows_w, w_pad)):
                    pool.indirect_dma_start(rows_of[:, c * 128:(c + 1) * 128], None, pad,
                                            bass.IndirectOffsetOnAxis(ap=tile_i[:, c:c + 1], axis=0),
                                            bounds_check=T - 1).then_inc(S.pair_rows, 16)

            due = pool.alloc_register("groups_used_due")

            def gathers(n):
                d, table, _, _ = PASSES[n]
                used = S.mixed if n == EDGE_MLP else S.part_ready
                base = 0 if n == EDGE_MLP else n * NG

                pool.wait_ge(S.table_stored, stored(n))

                pool.reg_mov(due, base + UG - 3)

                def body(i, q, t, last):
                    for g in range(UG):
                        if g % 2 == 0:
                            pool.wait_ge(S.idx_ready, n * (NP // 8) + t * 2 + g // 2 + 1)
                        if isinstance(q, int):
                            wait(pool, used, base + q + g - 3)
                        else:
                            pool.wait_ge(used, due)
                            pool.reg_add(due, due, 1)
                        for j in range(GR):
                            k = g * GR + j
                            pool.indirect_dma_start(G[:, k * d:(k + 1) * d], None, table,
                                                    bass.IndirectOffsetOnAxis(ap=idx_ring[:, k:k + 1], axis=0))\
                                .then_inc(gathered[k], 16)
                over_pairs(pool, body)

            pool.wait_ge(S.row0_ready, 1)
            pool.wait_ge(S.acc_zeroed, 16 * GR)

            def z_x(b, r):
                wait(pool, S.Z_xtr, b - 1)
                nc.gpsimd.tensor_copy(zs[0:PB, r, 0:D], node(X, b, D)).then_inc(S.Z_xs, 1)

            def z_h(b, r):
                pool.wait_ge(S.Z_h, b + 1)
                nc.gpsimd.tensor_tensor(node(HR, b, H), hs[0:PB, r, :], r_gb0[0:PB, :], ALU.add).then_inc(S.Z_hall, 1)
            over_blocks(pool, [(0, z_x), (5, z_h)])

            for l in range(L):
                gathers(l)
                sums_ended(pool, l)
                pool.wait_ge(S.weights_loaded, n_layer * 16 * (l + 1))

                def a_h(b, r):
                    pool.wait_ge(S.A_h, l * NB + b + 1)
                    nc.gpsimd.tensor_tensor(node(HR, b, H), hs[0:PB, r, :], r_be2[0:PB, :], ALU.add)\
                        .then_inc(S.A_hall, 1)
                over_blocks(pool, [(0, a_h)])
                if l < L - 1:
                    def c_h(b, r):
                        pool.wait_ge(S.C_h, l * NB + b + 1)
                        nc.gpsimd.tensor_tensor(node(HR, b, H), hs[0:PB, r, :], r_gb[0:PB, :], ALU.add)\
                            .then_inc(S.C_hall, 1)
                    over_blocks(pool, [(0, c_h)])

            def d_init(b, r):
                pool.wait_ge(S.D_x, b + 1)
                nc.gpsimd.tensor_copy(node(A, b, D), zs[0:PB, r, 0:D]).then_inc(S.D_init, 1)
            over_blocks(pool, [(0, d_init)])

            due_msg = pool.alloc_register("messages_due")
            due_scatter = [pool.alloc_register(f"scatters_due{j}") for j in range(GR)]
            pool.reg_mov(due_msg, UG + 1)
            for j in range(GR):
                pool.reg_mov(due_scatter[j], 16 * UG)

            def scatters(i, q, t, last):
                for g in range(UG):
                    if isinstance(q, int):
                        pool.wait_ge(S.R_msg, q + g + 1)
                        pool.wait_ge(S.R_idx, q + g + 1)
                    else:
                        pool.wait_ge(S.R_idx, q + g + 1)
                        pool.wait_ge(S.R_msg, due_msg)
                        pool.reg_add(due_msg, due_msg, 1)
                    for j in range(GR):
                        if isinstance(q, int):
                            wait(pool, scattered[j], 16 * (q + g))
                        else:
                            pool.wait_ge(scattered[j], due_scatter[j])
                            pool.reg_add(due_scatter[j], due_scatter[j], 16)
                        pool.indirect_dma_start(acc[j], bass.IndirectOffsetOnAxis(ap=s_idx[:, g, j:j + 1], axis=0),
                                                COMB[:, g, j, :], None, compute_op=ALU.add)\
                            .then_inc(scattered[j], 16)
            over_pairs(pool, scatters)
            for h, loaded in enumerate((S.acc_loaded0, S.acc_loaded1)):
                pool.wait_ge(loaded, 16 * 2 * GR)
                third = half(HR, h, H2)[0:PB, :]
                nc.gpsimd.tensor_tensor(third, third, half(X, h)[0:PB, :], ALU.add)\
                    .then_inc(S.S_sum, 1)

            def e_res(b, r):
                pool.wait_ge(S.E_x, b + 1)
                nc.gpsimd.tensor_tensor(node(X, b, D), zs[0:PB, r, 0:D], r_fb2[0:PB, :], ALU.add).then_inc(S.E_res, 1)
            over_blocks(pool, [(0, e_res)])
            gathers(L)
            sums_ended(pool, L)

            def f_r(b, r):
                wait(pool, S.F_tr, b - 1)
                nc.gpsimd.tensor_copy(zs[0:PB, r, 0:D], node(HR, b, D, H2)).then_inc(S.F_r, 1)
            over_blocks(pool, [(0, f_r)])

            gathers(L + 1)
            for c in range(NCH + 2):
                if c < NCH:
                    pool.wait_ge(S.H_o, c + 1)
                    nc.gpsimd.tensor_tensor(chunk(HR, c, D), chunk(HR, c, D), per_feature(r_l3b, D), ALU.add)\
                        .then_inc(S.H_b, 1)
                if c >= 2:
                    pool.wait_ge(S.H_p, c - 1)
                    nc.gpsimd.tensor_tensor(chunk(A, c - 2, D), chunk(HR, c - 2, D), chunk(X, c - 2, D), ALU.add)\
                        .then_inc(S.H_v, 1)
            for c in range(NCH):
                pool.wait_ge(S.I_m, c + 1)
                nc.gpsimd.tensor_tensor(chunk(A, c, D, A2), chunk(HR, c, D), per_node(ln[:, 7, :], c, D), ALU.add)\
                    .then_inc(S.I_o, 1)

        @block.scalar
        def _(act):
            def act_fn(out_, in_, f, **k):
                return nc.scalar.activation(out_, in_, f, **k)

            def evacuate(tr, base, dst, free, done, d):
                def stage(b, r):
                    act.wait_ge(tr, base + b + 1)
                    wait(act, free, base + b - 1)
                    nc.scalar.copy(dst[:, r, 0:d // 128, :], PS[:, r, 0:d // 128 * 128]
                                   .rearrange("p (k n) -> p k n", n=128)[:, :, 0:PB]).then_inc(done, 1)
                return stage

            def scaled(ps, base, buf, at, d, done):
                def stage(b, r):
                    act.wait_ge(ps, base + b + 1)
                    act_fn(node(buf, b, d, at), PS[0:PB, 2 + r, 0:d], ACT.Copy, scale=column(dinv, b))\
                        .then_inc(done, 1)
                return stage

            def normed(buf, at, d, base, free, done, width=None):
                def stage(b, r):
                    for f in free:
                        wait(act, f, base + b - 1)
                    act_fn(zs[0:PB, r, 0:d], node(buf, b, d, at), ACT.Identity, scale=column(rstd, b),
                           bias=column(nmr, b)).then_inc(done, 1)
                return stage

            def root(k, d=D):
                act.wait_ge(S.sqrt_in, k + 2)
                act_fn(ln[0:PB, 5, :], ln[0:PB, 4, :], ACT.Sqrt, scale=1.0 / d, bias=eps[0:PB, :])\
                    .then_inc(S.sqrt_out, 1)
                act.wait_ge(S.rstd_ready, k + 1)

            def indices(n):
                used = S.mixed if n == EDGE_MLP else S.part_ready
                base = 0 if n == EDGE_MLP else n * NG

                def idx(i, q, h):
                    wait(act, used, base + q + 2 * h - 2)
                    nc.scalar.copy(idx_ring[:, 8 * h:8 * h + 8], span(srcP, i + 8 * h, 8)).then_inc(S.idx_ready, 1)
                if n == EDGE_MLP:
                    return idx

                def body(i, q, t, last):
                    for h in range(2):
                        idx(i, q, h)
                if n:
                    sums_ended(act, n - 1)
                else:
                    act.wait_ge(S.pairs_ready, 4)
                over_pairs(act, body)

            act.wait_ge(S.te_s, 1)
            act_fn(c_ts[:, :], c_ts[:, :], ACT.Silu).then_inc(S.te_s, 1)
            act.wait_ge(S.te_s, 5)
            act.wait_ge(S.row0_ready, 1)
            act.wait_ge(S.pairs_ready, 5)

            def counted(b, r):
                act.wait_ge(S.deg_used, b + 1)
                nc.scalar.copy(span(counts[0:PB, :], b * 16, 16), PS[0:PB, 5, 0:16]).then_inc(S.deg_counted, 1)

            def z_xt(b, r):
                act.wait_ge(S.Z_xtr, b + 1)
                wait(act, S.Z_hps, b - 1)
                nc.scalar.copy(uT[:, r, 0, :], PS[:, 4, 0:PB]).then_inc(S.Z_xt, 1)

            def z_yu(b, r):
                act.wait_ge(S.Z_yps, b + 1)
                nc.scalar.copy(node(A, b, H), PS[0:PB, 2 + r, 0:H]).then_inc(S.Z_yu, 1)
            over_blocks(act, [(8, z_yu), (6, evacuate(S.Z_htr, 0, hT, S.Z_yps, S.Z_ht, H)), (2, z_xt), (1, counted)])
            for b in range(NB, NP // 16):
                counted(b, 0)
            act.wait_ge(S.sqrt_in, 1)
            act_fn(dsq[0:PB, :], dsq[0:PB, :], ACT.Sqrt).then_inc(S.sqrt_out, 1)
            act.wait_ge(S.dinv_ready, 1)
            for l in range(L):
                base = l * NB
                indices(l)
                sums_ended(act, l)
                over_blocks(act, [(2, evacuate(S.A_tr, base, hT, S.A_ps, S.A_ht, H))])
                root(2 * l, H)

                def b_silu(b, r):
                    act.wait_ge(S.B_tr, base + b + 1)
                    wait(act, S.B_ps, base + b - 1)
                    for k in range(2):
                        ins = act_fn(hT[:, r, k, :], PS[:, r, k * 128:k * 128 + PB], ACT.Silu, scale=c_g1[:, k:k + 1],
                                     bias=c_be1[:, k:k + 1])
                    ins.then_inc(S.B_rt, 1)
                over_blocks(act, [(2, b_silu)])
                root(2 * l + 1, H)
                if l < L - 1:
                    over_blocks(act, [(6, scaled(S.C_yps, base, A, 0, H, S.C_y)),
                                      (4, evacuate(S.C_tr, base, hT, S.C_yps, S.C_ht, H))])

            def m_ut(b, r):
                act.wait_ge(S.M_ups, b + 1)
                wait(act, S.M_ops, b - 1)
                for k in range(2):
                    ins = act_fn(uT[:, r, k, :], PS[:, 6 + r, k * 128:k * 128 + PB], ACT.Silu, bias=c_ob1[:, k:k + 1])
                ins.then_inc(S.M_ut, 1)
            over_blocks(act, [(6, m_ut), (4, evacuate(S.M_tr, 0, hT, S.M_ups, S.M_ht, H))])
            root(2 * L)
            over_blocks(act, [(2, evacuate(S.D_tr, 0, hT, S.D_ps, S.D_xt, D))])
            phase_ended(act, "D")

            def r_cols(q, r):
                wait(act, S.R_same, q - 3)
                wait(act, S.R_rows, q - 3)
                wait(act, S.R_idx, q - 3)
                nc.scalar.copy(s_col[:, r, :], span(srcP, q * GR, GR)).then_inc(S.R_cols, 1)
                nc.scalar.copy(w_col[:, r, :], span(wP, q * GR, GR)).then_inc(S.R_cols, 1)

            def r_ct(q, r):
                act.wait_ge(S.R_comb, q + 1)
                wait(act, S.R_mixed, q - 1)
                nc.scalar.copy(OHT[0:PB, r, :, :], PS[0:PB, 2 + r, :].rearrange("p (j e) -> p j e", j=GR))\
                    .then_inc(S.R_ct, 1)

            def r_msg(q, r, slot):
                act.wait_ge(S.R_mixed, q + 1)
                for j in range(GR):
                    wait(act, scattered[j], 0 if isinstance(q, int) and q < 4 else 16 * (q - 3))
                nc.scalar.copy(COMB[:, slot, :, :], PS[:, 4 + r, :].rearrange("p (j c) -> p j c", j=GR))\
                    .then_inc(S.R_msg, 1)

            def r_body(i, first, t, last):
                for g in range(UG):
                    q = first + g
                    if not last or g + 1 < UG:
                        r_ct(q + 1, (g + 1) % 2)
                    if not last or g + 3 < UG:
                        r_cols(q + 3, (g + 3) % 4)
                    r_msg(q, g % 2, g)
            r_cols(0, 0)
            r_cols(1, 1)
            r_cols(2, 2)
            r_ct(0, 0)
            over_pairs(act, r_body)
            root(2 * L + 1)

            def e_p(b, r):
                act.wait_ge(S.E_ps, b + 1)
                nc.scalar.copy(node(A, b, D, A2), PS[0:PB, 2 + r, 0:D]).then_inc(S.E_p, 1)
            over_blocks(act, [(4, e_p), (2, evacuate(S.E_tr, 0, hT, S.E_ps, S.E_xt, D)),
                              (0, normed(A, 0, D, 0, [S.E_tr, S.E_res, S.E_init], S.E_x))])
            phase_ended(act, "E")
            idx = indices(L)

            def oht(g, r):
                act.wait_ge(S.oht_ps, g + 1)
                wait(act, S.mixed, g - 1)
                nc.scalar.copy(OHT[0:PB, r, :, :], PS[0:PB, 4 + r, :].rearrange("p (j e) -> p j e", j=GR))\
                    .then_inc(S.oht_ready, 1)

            def relu(g, r):
                act.wait_ge(S.mixed, g + 1)
                wait(act, S.part_ready, L * NG + g - 1)
                act_fn(MSG[:, r, :, :], PS[:, 6 + r, :].rearrange("p (j c) -> p j c", j=GR), ACT.Relu)\
                    .then_inc(S.msg_ready, 1)

            def mlp_body(i, first, t, last):
                for g in range(UG):
                    q = first + g
                    if g == 0:
                        idx(i, first, 1)
                    if g == 2 and not last:
                        idx(i + U, first + UG, 0)
                    if not last or g + 1 < UG:
                        oht(q + 1, (g + 1) % 2)
                    relu(q, g % 2)
            idx(0, 0, 0)
            oht(0, 0)
            over_pairs(act, mlp_body)
            sums_ended(act, L)

            def f_ut(b, r):
                act.wait_ge(S.F_ups, b + 1)
                wait(act, S.F_ops, b - 1)
                act_fn(uT[:, r, 0, :], PS[:, 6 + r, 0:PB], ACT.Relu, bias=c_fb1[:, 0:1]).then_inc(S.F_ut, 1)
            over_blocks(act, [(4, f_ut), (2, evacuate(S.F_tr, 0, hT, S.F_ups, S.F_rt, D))])
            root(2 * L + 2)
            over_blocks(act, [(4, scaled(S.G_ps, 0, A, A2, D, S.G_y)),
                              (2, evacuate(S.G_tr, 0, hT, S.G_ps, S.G_xt, D))])
            indices(L + 1)
            root(2 * L + 3)

        @block.tensor
        def _(pe):
            def transposed(ready, base, src, d, free, done, bank=0):
                def stage(b, r):
                    pe.wait_ge(ready, base + b + 1)
                    wait(pe, free, base + b - 1)
                    for k in range(d // 128):
                        ins = nc.tensor.transpose(PS[:, bank + r, k * 128:k * 128 + PB],
                                                  src[0:PB, r, k * 128:(k + 1) * 128], ident[0:PB, 0:PB])
                    ins.then_inc(done, 1)
                return stage

            def product(ready, base, w, ks, d, free, done, src=None, bank=2):
                src = hT if src is None else src

                def stage(b, r):
                    pe.wait_ge(ready, base + b + 1)
                    wait(pe, free, base + b - 1)
                    for k in range(ks):
                        ins = nc.tensor.matmul(PS[0:PB, bank + r, 0:d], src[:, r, k, :], w(k),
                                               start=(k == 0), stop=(k == ks - 1))
                    ins.then_inc(done, 1)
                return stage

            def product_t(ready, base, w, ks, ms, free, done):
                def stage(b, r):
                    pe.wait_ge(ready, base + b + 1)
                    wait(pe, free, base + b - 1)
                    for m in range(ms):
                        for k in range(ks):
                            ins = nc.tensor.matmul(PS[:, 6 + r, m * 128:m * 128 + PB], w(k, m), hT[:, r, k, :],
                                                   start=(k == 0), stop=(k == ks - 1))
                    ins.then_inc(done, 1)
                return stage

            def segment_sums(n):
                d = PASSES[n][0]

                def body(i, first, t, last):
                    for g in range(UG):
                        q = n * NG + first + g
                        pe.wait_ge(S.onehot_ready, q + 1)
                        wait(pe, S.acc_done, n * NP + i + (g - 1) * GR)
                        for j in range(GR):
                            k = g * GR + j
                            pe.wait_ge(gathered[k], 16 * (n * (NP // U) + 1) + i)
                            ins = nc.tensor.matmul(part(g % 2, d)[:, j, :], OH[:, g, j, :], G[:, k * d:(k + 1) * d],
                                                   start=True, stop=True)
                        ins.then_inc(S.part_ready, 1)
                over_pairs(pe, body)

            def edge_messages():
                n = EDGE_MLP

                def turn(q, g):
                    pe.wait_ge(S.onehot_ready, n * NG + q + 1)
                    wait(pe, S.oht_ready, q - 1)
                    for j in range(GR):
                        ins = nc.tensor.transpose(PS[0:PB, 4 + g % 2, j * 128:(j + 1) * 128], OH[:, g % 4, j, :],
                                                  ident[:, :])
                    ins.then_inc(S.oht_ps, 1)

                def mix(q, g, i):
                    word = nc.tensor.value_load(span(bpack, q, 1))
                    pe.wait_ge(S.oht_ready, q + 1)
                    wait(pe, S.msg_ready, q - 1)
                    for j in range(GR):
                        k = g * GR + j
                        pe.wait_ge(gathered[k], 16 * (n * (NP // U) + 1) + i)
                        nc.tensor.matmul(PS[:, 6 + g % 2, j * D:(j + 1) * D], OHT[0:PB, g % 2, j, :],
                                         HR[0:PB, bass.ds(block_at(pe, word, j, D), D)], start=True, stop=False)
                        ins = nc.tensor.matmul(PS[:, 6 + g % 2, j * D:(j + 1) * D], ident[:, :],
                                               G[:, k * D:(k + 1) * D], start=False, stop=True)
                    ins.then_inc(S.mixed, 1)

                def add(q, g):
                    pe.wait_ge(S.msg_ready, q + 1)
                    wait(pe, S.acc_done, n * NP + q * GR - GR)
                    for j in range(GR):
                        ins = nc.tensor.matmul(part(g % 2, D)[:, j, :], OH[:, g % 4, j, :], MSG[:, g % 2, j, :],
                                               start=True, stop=True)
                    ins.then_inc(S.part_ready, 1)

                def body(i, first, t, last):
                    for g in range(UG):
                        q = first + g
                        if not last or g + 1 < UG:
                            turn(q + 1, g + 1)
                        mix(q, g, i)
                        if not isinstance(q, int) or q >= 1:
                            add(q - 1, (g - 1) % 4)
                turn(0, 0)
                over_pairs(pe, body)
                add(NG - 1, 3)

            pe.wait_ge(S.consts, 5)
            for c in range(NC):
                ins = nc.tensor.transpose(PSF[:, c * 128:(c + 1) * 128], cols[:, 0, c:c + 1].broadcast_to([128, 128]),
                                          ident[:, :])
            ins.then_inc(S.keys_transposed, 1)
            pe.wait_ge(S.keyrow_ready, 2)
            for t, v in enumerate((rows_d, rows_s, rows_w)):
                for c in range(NC):
                    nc.tensor.transpose(PSF[:, t * 896 + c * 128:t * 896 + (c + 1) * 128],
                                        v[:, c * 128:(c + 1) * 128], ident[:, :])
            for c in range(NC):
                ins = nc.tensor.transpose(PSF[:, 2688 + c * 128:2688 + (c + 1) * 128],
                                          cols[:, 2, c:c + 1].broadcast_to([128, 128]), ident[:, :])
            ins.then_inc(S.pairs_transposed, 1)
            pe.wait_ge(S.pairs_ready, 4)
            pe.wait_ge(S.te_s, 4)
            for k in range(2):
                ins = nc.tensor.matmul(PS[0:PB, 1, 0:H], te_l[:, k, :], w_t2[:, k, :], start=(k == 0), stop=(k == 1))
            ins.then_inc(S.te_ps, 1)
            pe.wait_ge(S.row0_ready, 1)

            def deg_steps(b, r):
                for h in range(2):
                    pe.wait_ge(S.deg_nodes, 2 * b + h + 1)
                    if h == 0:
                        wait(pe, S.deg_counted, b)
                    for j in range(8):
                        ins = nc.tensor.matmul(PS[0:PB, 5, 8 * h + j:8 * h + j + 1], deg_n[:, r, h, :, j], ones[:, :],
                                               start=True, stop=True)
                ins.then_inc(S.deg_used, 1)

            def z_xtr(b, r):
                pe.wait_ge(S.Z_xs, b + 1)
                wait(pe, S.Z_xt, b)
                nc.tensor.transpose(PS[:, 4, 0:PB], zs[0:PB, r, 0:D], ident[0:PB, 0:PB]).then_inc(S.Z_xtr, 1)
            over_blocks(pe, [(7, product(S.Z_ht, 0, lambda k: w_g0[:, k, :], 2, H, S.Z_yu, S.Z_yps)),
                             (5, transposed(S.Z_h, 0, hs, H, S.Z_ht, S.Z_htr)),
                             (3, product(S.Z_xt, 0, lambda k: w_in[:, :], 1, H, S.Z_h, S.Z_hps, uT, 6)),
                             (1, z_xtr), (0, deg_steps)])
            for b in range(NB, NP // 16):
                deg_steps(b, b % 2)
            pe.wait_ge(S.Z_yu, NB)
            pe.wait_ge(S.deg_counted, NP // 16)
            for c in range(NC):
                n = min(128, NP - c * 128)
                ins = nc.tensor.transpose(PSF[0:n, c * 128:c * 128 + PB], counts[0:PB, c * 128:c * 128 + n],
                                          ident[0:PB, 0:PB])
            ins.then_inc(S.deg_tr, 1)
            pe.wait_ge(S.deg_lhs, 3)
            for c in range(NC):
                n = min(128, NP - c * 128)
                ins = nc.tensor.matmul(PS[0:PB, 5, 0:NB], count_t[0:n, c, :], pair_block[0:n, c, :], start=(c == 0),
                                       stop=(c == NC - 1))
            ins.then_inc(S.deg_sum, 1)
            for l in range(L):
                base = l * NB
                phase_ended(pe, "Z") if l == 0 else phase_ended(pe, "C", l - 1)
                segment_sums(l)
                sums_ended(pe, l)
                pe.wait_ge(S.weights_loaded, n_layer * 16 * (l + 1))
                over_blocks(pe, [(3, product(S.A_ht, base, lambda k: w_a[:, k, :], 2, H, S.A_t, S.A_ps)),
                                 (1, transposed(S.A_h, base, hs, H, S.A_ht, S.A_tr))])
                over_blocks(pe, [(3, product(S.B_rt, base, lambda k: w_b[:, k, :], 2, H, S.B_t, S.B_ps)),
                                 (1, transposed(S.B_z, base, zs, H, S.B_rt, S.B_tr))])
                if l < L - 1:
                    over_blocks(pe, [(5, product(S.C_ht, base, lambda k: w_c[:, k, :], 2, H, S.C_y, S.C_yps)),
                                     (3, transposed(S.C_h, base, hs, H, S.C_ht, S.C_tr))])
            over_blocks(pe, [(7, product(S.M_ut, 0, lambda k: w_o2[:, k, :], 2, D, S.M_v, S.M_ops, uT, 4)),
                             (5, product_t(S.M_ht, 0, lambda k, m: w_o1[:, k, m * 128:(m + 1) * 128], 2, 2, S.M_ut,
                                           S.M_ups)),
                             (3, transposed(S.M_h, 0, hs, H, S.M_ht, S.M_tr))])
            over_blocks(pe, [(3, product(S.D_xt, 0, lambda k: w_l1[:, :], 1, D, S.D_y, S.D_ps)),
                             (1, transposed(S.D_x, 0, zs, D, S.D_xt, S.D_tr))])
            phase_ended(pe, "D")

            def r_rows(q, r, slot):
                pe.wait_ge(S.R_cols, 2 * q + 2)
                wait(pe, S.R_same, q - 1)
                for j in range(GR):
                    ins = nc.tensor.transpose(PS[:, r, j * 128:(j + 1) * 128],
                                              s_col[:, slot, j:j + 1].broadcast_to([128, 128]), ident[:, :])
                ins.then_inc(S.R_rows, 1)

            def r_comb(q, r, slot):
                pe.wait_ge(S.R_onehot, q + 1)
                pe.wait_ge(S.R_same, q + 1)
                wait(pe, S.R_ct, q - 1)
                for j in range(GR):
                    ins = nc.tensor.matmul(PS[0:PB, 2 + r, j * 128:(j + 1) * 128], OH[:, slot, j, :],
                                           SAME[:, r, j, :], start=True, stop=True)
                ins.then_inc(S.R_comb, 1)

            def r_mix(q, r):
                word = nc.tensor.value_load(span(bpack, q, 1))
                pe.wait_ge(S.R_ct, q + 1)
                wait(pe, S.R_msg, q - 1)
                for j in range(GR):
                    ins = nc.tensor.matmul(PS[:, 4 + r, j * D:(j + 1) * D], OHT[0:PB, r, j, :],
                                           HR[0:PB, bass.ds(block_at(pe, word, j, D), D)], start=True, stop=True)
                ins.then_inc(S.R_mixed, 1)

            def r_body(i, first, t, last):
                for g in range(UG):
                    q = first + g
                    if not last or g + 2 < UG:
                        r_rows(q + 2, g % 2, (g + 2) % 4)
                    if not last or g + 1 < UG:
                        r_comb(q + 1, (g + 1) % 2, (g + 1) % 4)
                    r_mix(q, g % 2)
            r_rows(0, 0, 0)
            r_rows(1, 1, 1)
            r_comb(0, 0, 0)
            over_pairs(pe, r_body)
            for j in range(GR):
                pe.wait_ge(scattered[j], 16 * NG)
            def e_product(b, r):
                pe.wait_ge(S.E_xt, b + 1)
                wait(pe, S.E_p, b - 1)
                wait(pe, S.E_q, b - 1)
                for k in range(2):
                    ins = nc.tensor.matmul(PS[0:PB, 2 + 4 * k + r, 0:D], hT[:, r, 0, :], w_e[:, k, :], start=True,
                                           stop=True)
                ins.then_inc(S.E_ps, 1)
            over_blocks(pe, [(3, e_product), (1, transposed(S.E_x, 0, zs, D, S.E_xt, S.E_tr))])
            phase_ended(pe, "E")
            edge_messages()
            sums_ended(pe, L)
            over_blocks(pe, [(5, product(S.F_ut, 0, lambda k: w_f2[:, :], 1, D, S.F_v, S.F_ops, uT, 4)),
                             (3, product_t(S.F_rt, 0, lambda k, m: w_f1[:, :], 1, 1, S.F_ut, S.F_ups)),
                             (1, transposed(S.F_r, 0, zs, D, S.F_rt, S.F_tr))])
            over_blocks(pe, [(3, product(S.G_xt, 0, lambda k: w_l3[:, :], 1, D, S.G_y, S.G_ps)),
                             (1, transposed(S.G_x, 0, zs, D, S.G_xt, S.G_tr))])
            phase_ended(pe, "G")
            segment_sums(L + 1)

        @block.vector
        def _(dve):
            chained = [0]

            def link(ins):
                chained[0] += 1
                ins.then_inc(S.chain_dve, 1)
                dve.wait_ge(S.chain_dve, chained[0])

            v = nc.vector

            def norm(k, d):
                st = stats[0:PB, :, :]
                me, se, mo, so = st[:, :, 1], st[:, :, 2], st[:, :, 4], st[:, :, 5]
                w = [ln[0:PB, q, :] for q in range(8)]
                v.tensor_tensor(w[3], se, so, ALU.add).then_inc(S.chain_dve, 1)
                chained[0] += 1
                link(v.tensor_tensor(w[1], me, mo, ALU.subtract))
                link(v.scalar_tensor_tensor(w[2], w[1], 0.25 * d, w[1], ALU.mult, ALU.mult))
                v.tensor_tensor(w[4], w[3], w[2], ALU.add).then_inc(S.sqrt_in, 1)
                link(v.tensor_tensor(w[0], me, mo, ALU.add))
                dve.wait_ge(S.sqrt_out, k + 2)
                link(v.reciprocal(rstd, w[5]))
                v.scalar_tensor_tensor(nmr, w[0], -0.5, rstd, ALU.mult, ALU.mult).then_inc(S.rstd_ready, 1)
                dve.wait_ge(S.rstd_ready, k + 1)

            def sums(n):
                d, _, buf, at = PASSES[n]

                def onehots(i, first, g):
                    q = first + g
                    slot = g % 4
                    wait(dve, S.part_ready, n * NG + q - 3)
                    st = i + g * GR
                    ins = v.tensor_tensor(OH[:, slot, :, :], iota[:, 0:PB].unsqueeze(1).broadcast_to([128, GR, PB]),
                                          span(dlP, st, GR).unsqueeze(2).broadcast_to([128, GR, PB]), ALU.is_equal)
                    ins.then_inc(S.onehot_ready, 1)
                onehots(0, 0, 0)
                onehots(0, 0, 1)
                onehots(0, 0, 2)
                dve.wait_ge(S.table_stored, stored(n))

                def body(i, first, t, last):
                    for g in range(UG):
                        if not last or g + 3 < UG:
                            onehots(i, first, g + 3)
                        word = v.value_load(span(bpack, first + g, 1))
                        dve.wait_ge(S.part_ready, n * NG + first + g + 1)
                        for j in range(GR):
                            off = block_at(dve, word, j, d)
                            here = buf[0:PB, bass.ds(off + at, d)]
                            wait(dve, S.acc_done, n * NP + i + g * GR + j)
                            v.tensor_tensor(here, part(g % 2, d)[:, j, :], here, ALU.add).then_inc(S.acc_done, 1)
                over_pairs(dve, body)
                sums_ended(dve, n)

            dve.wait_ge(S.lasts_loaded, 32)
            dve.wait_ge(S.consts, 4)
            link(v.tensor_copy(iota[:, :], iota_i[:, :]))
            link(v.tensor_copy(thr[:, :], thr_i[:, :]))
            link(v.tensor_copy(pcol[:, :], pcol_i[:, :]))
            link(v.memset(dlast[:, :], float(FAR)))
            full = T // 128
            link(v.tensor_copy(dlast[:, 0:full], dlast_i[:, 0:full]))
            link(v.tensor_copy(dlast[0:T - full * 128, full:full + 1], dlast_i[0:T - full * 128, full:full + 1]))
            for c in range(NC):
                link(v.tensor_scalar(junk[:, 0:NB - 1], thr[:, :], dlast[:, c:c + 1], None, ALU.is_le, ALU.add,
                                     accum_out=cols[:, 1, c:c + 1]))
            v.tensor_tensor(cols[:, 0, :], cols[:, 1, :], pcol[:, :], ALU.add).then_inc(S.consts, 1)
            dve.wait_ge(S.keys_transposed, 1)
            link(v.tensor_copy(keyrow, PSF[:, 0:NC * 128]))
            for c in range(NC):
                link(v.tensor_scalar(junk[:, 0:T], keyrow[:, 0:T], pcol[:, c:c + 1], None, ALU.is_lt, ALU.add,
                                     accum_out=cols[:, 1, c:c + 1]))
            link(v.tensor_scalar(cols[:, 1, :], cols[:, 1, :], float(T - 1), None, ALU.min))
            v.tensor_copy(tile_i[:, :], cols[:, 1, :]).then_inc(S.pair_tiles, 1)
            link(v.tensor_tensor(cols[:, 2, :], pcol[:, :], cols[:, 1, :], ALU.subtract))
            link(v.tensor_scalar(cols[:, 3, :], cols[:, 2, :], float(PB), None, ALU.mult))
            dve.wait_ge(S.pair_rows, 16 * 3 * NC)
            v.tensor_copy(rows_s, rows_si).then_inc(S.keyrow_ready, 1)
            v.tensor_tensor(rows_d.rearrange("p (c e) -> p c e", c=NC), rows_di.rearrange("p (c e) -> p c e", c=NC),
                            cols[:, 3, :].unsqueeze(2).broadcast_to([128, NC, 128]), ALU.subtract)\
                .then_inc(S.keyrow_ready, 1)
            dve.wait_ge(S.pairs_transposed, 1)
            v.tensor_copy(dlP[:, :], PSF[:, 0:NP]).then_inc(S.pairs_ready, 1)
            v.tensor_copy(srcP[:, :], PSF[:, 896:896 + NP]).then_inc(S.pairs_ready, 1)
            v.tensor_copy(wP[:, :], PSF[:, 1792:1792 + NP]).then_inc(S.pairs_ready, 1)
            v.tensor_copy(brow, PSF[:, 2688:2688 + NC * 128]).then_inc(S.pairs_ready, 1)
            dve.wait_ge(S.pairs_ready, 4)
            link(v.tensor_scalar(bpack_f, brow[0:1, 0:NP], float(NB - 1), None, ALU.min))
            four = bpack_f.rearrange("p (g j) -> p g j", j=GR)
            for j in range(GR - 1, 1, -1):
                link(v.scalar_tensor_tensor(four[:, :, j - 1], four[:, :, j], 64.0, four[:, :, j - 1], ALU.mult,
                                            ALU.add))
            v.scalar_tensor_tensor(bpack[:, :], four[:, :, 1], 64.0, four[:, :, 0], ALU.mult, ALU.add)\
                .then_inc(S.pairs_ready, 1)
            dve.wait_ge(S.pairs_ready, 5)

            dve.wait_ge(S.loaded, n_first * 16)
            v.scalar_tensor_tensor(c_ts[:, :], c_tw1[:, :], c_t[:, 0:1], c_tb1[:, :], ALU.mult, ALU.add)\
                .then_inc(S.te_s, 1)
            dve.wait_ge(S.te_s, 2)
            v.tensor_copy(te_l[:, :, :], c_ts[:, :].unsqueeze(2).broadcast_to([128, 2, PB])).then_inc(S.te_s, 1)
            link(v.tensor_tensor(r_row0[:, :], r_row0[:, :], r_tb2[:, :], ALU.add))
            v.memset(ones[:, :], 1.0).then_inc(S.te_s, 1)
            v.memset(eps[:, :], EPS).then_inc(S.te_s, 1)
            link(v.tensor_scalar(onepe[:, :], c_eps[:, :], 1.0, None, ALU.add))
            dve.wait_ge(S.te_ps, 1)
            v.tensor_tensor(r_row0[0:PB, :], PS[0:PB, 1, 0:H], r_row0[0:PB, :], ALU.add).then_inc(S.row0_ready, 1)
            dve.wait_ge(S.row0_ready, 1)

            link(v.tensor_copy(dl16, dlP[:, :]))
            link(v.tensor_copy(iota_x, iota[:, 0:PB].unsqueeze(2).broadcast_to([128, PB, 8])))

            def deg_step(q, b, r, h):
                wait(dve, S.deg_used, b - 1)
                v.tensor_tensor(deg_n[:, r, h, :, :], iota_x,
                                span(dl16, q * 8, 8).unsqueeze(1).broadcast_to([128, PB, 8]), ALU.is_equal)\
                    .then_inc(S.deg_nodes, 1)

            def deg_steps(b, r):
                deg_step(2 * b, b, r, 0)
                deg_step(2 * b + 1, b, r, 1)

            def z_h(b, r):
                dve.wait_ge(S.Z_hps, b + 1)
                wait(dve, S.Z_htr, b - 1)
                wait(dve, S.Z_hall, b - 1)
                v.tensor_tensor(hs[0:PB, r, :], PS[0:PB, 6 + r, 0:H], r_row0[0:PB, :], ALU.add).then_inc(S.Z_h, 1)
            over_blocks(dve, [(0, deg_steps), (4, z_h)])
            for b in range(NB, NP // 16):
                deg_steps(b, b % 2)
            v.tensor_tensor(pair_block, iota[:, 0:NB].unsqueeze(1).broadcast_to([128, NC, NB]),
                            cols[:, 2, :].unsqueeze(2).broadcast_to([128, NC, NB]), ALU.is_equal).then_inc(S.deg_lhs, 1)
            dve.wait_ge(S.deg_tr, 1)
            counted = PSF[:, 0:NC * 128].rearrange("p (c n) -> p c n", n=128)
            full, n = NP // 128, NP % 128
            v.tensor_copy(count_t[:, 0:full, :], counted[:, 0:full, 0:PB]).then_inc(S.deg_lhs, 1)
            v.tensor_copy(count_t[0:n, full, :], counted[0:n, full, 0:PB]).then_inc(S.deg_lhs, 1)
            dve.wait_ge(S.deg_sum, 1)
            v.tensor_scalar(dsq[0:PB, :], PS[0:PB, 5, 0:NB], 1.0, None, ALU.add).then_inc(S.sqrt_in, 1)
            dve.wait_ge(S.sqrt_out, 1)
            v.reciprocal(dinv[0:PB, :], dsq[0:PB, :]).then_inc(S.dinv_ready, 1)
            dve.wait_ge(S.dinv_ready, 1)
            dve.wait_ge(S.Z_yu, NB)
            for c in range(NCH):
                v.tensor_tensor(chunk(A, c, H), chunk(A, c, H), per_node(dinv, c, H), ALU.mult).then_inc(S.Z_y, 1)
            dve.wait_ge(S.Z_xs, NB)
            every = X[0:PB, :].rearrange("p (b d) -> p b d", d=D)
            v.tensor_tensor(every, every, r_ob2[0:PB, :].unsqueeze(1).broadcast_to([PB, NB, D]), ALU.add)\
                .then_inc(S.Z_x, 1)
            dve.wait_ge(S.Z_x, 1)

            def biased(lag, ps, base, brow_, d, done, counted, buf=None, at=0, res=None, bank=2):
                buf = A if buf is None else buf

                def stage(b, r):
                    dve.wait_ge(ps, base + b + 1)
                    other = brow_[0:PB, :] if res is None else node(res, b, d)
                    v.tensor_tensor(node(buf, b, d, at), PS[0:PB, bank + r, 0:d], other, ALU.add).then_inc(done, 1)

                def count(b, r):
                    dve.wait_ge(done, base + b + 1)
                    v.bn_stats(stat(b), node(buf, b, d, at)).then_inc(counted, 1)
                return [(lag + 1, count), (lag, stage)]

            def normed(buf, d, base, free, done):
                def stage(b, r):
                    for f in free:
                        wait(dve, f, base + b - 1)
                    v.tensor_scalar(zs[0:PB, r, 0:d], node(buf, b, d), column(rstd, b), column(nmr, b), ALU.mult,
                                    ALU.add).then_inc(done, 1)
                return stage

            def new_h(lag, base, z, q_, h_, tr, hall):
                def gain(b, r):
                    dve.wait_ge(z, base + b + 1)
                    wait(dve, h_, base + b - 1)
                    v.tensor_tensor(qs[0:PB, r, :], zs[0:PB, r, :], r_g2[0:PB, :], ALU.mult).then_inc(q_, 1)

                def total(b, r):
                    dve.wait_ge(q_, base + b + 1)
                    wait(dve, tr, base + b - 1)
                    if hall is not None:
                        wait(dve, hall, base + b - 1)
                    v.tensor_tensor(hs[0:PB, r, :], qs[0:PB, r, :], node(HR, b, H), ALU.add).then_inc(h_, 1)
                return [(lag + 1, total), (lag, gain)]

            for l in range(L):
                base = l * NB
                sums(l)
                dve.wait_ge(S.weights_loaded, n_layer * 16 * (l + 1))

                def a_h(b, r):
                    wait(dve, S.A_tr, base + b - 1)
                    wait(dve, S.A_hall, base + b - 1)
                    v.scalar_tensor_tensor(hs[0:PB, r, :], node(A, b, H), column(dinv, b), node(HR, b, H), ALU.mult,
                                           ALU.add).then_inc(S.A_h, 1)
                over_blocks(dve, biased(4, S.A_ps, base, r_b1, H, S.A_t, S.A_stat) + [(0, a_h)])
                phase_ended(dve, "A", l)
                norm(2 * l, H)
                over_blocks(dve, biased(4, S.B_ps, base, r_b2, H, S.B_t, S.B_stat)
                            + [(0, normed(A, H, base, [S.B_tr], S.B_z))])
                phase_ended(dve, "B", l)
                norm(2 * l + 1, H)
                if l < L - 1:
                    over_blocks(dve, new_h(1, base, S.C_z, S.C_q, S.C_h, S.C_tr, S.C_hall)
                                + [(0, normed(A, H, base, [S.C_q], S.C_z))])
            over_blocks(dve, biased(8, S.M_ops, 0, None, D, S.M_v, S.M_stat, X, 0, X, 4)
                        + new_h(1, 0, S.M_z, S.M_q, S.M_h, S.M_tr, None) + [(0, normed(A, H, 0, [S.M_q], S.M_z))])
            phase_ended(dve, "M")
            norm(2 * L, D)

            def d_y(b, r):
                dve.wait_ge(S.D_ps, b + 1)
                v.tensor_tensor(node(HR, b, D), PS[0:PB, 2 + r, 0:D], r_l1b[0:PB, :], ALU.add).then_inc(S.D_y, 1)
            over_blocks(dve, [(4, d_y), (0, normed(X, D, 0, [S.D_tr, S.D_init], S.D_x))])
            phase_ended(dve, "D")
            link(v.tensor_scalar(before[:, :], iota[:, :], pcol[:, 0:1], None, ALU.is_lt))
            link(v.tensor_scalar(trash[:, :], pcol[:, 0:1], float(N), None, ALU.add))

            def r_onehots(q, slot):
                wait(dve, S.R_comb, q - 3)
                v.tensor_tensor(OH[:, slot, :, :], iota[:, 0:PB].unsqueeze(1).broadcast_to([128, GR, PB]),
                                span(dlP, q * GR, GR).unsqueeze(2).broadcast_to([128, GR, PB]), ALU.is_equal)\
                    .then_inc(S.R_onehot, 1)

            def r_same(q, r, slot):
                dve.wait_ge(S.R_rows, q + 1)
                wait(dve, S.R_comb, q - 1)
                for j in range(GR):
                    row_j = PS[:, r, j * 128:(j + 1) * 128]
                    v.scalar_tensor_tensor(products[:, r, j, :], row_j, s_col[:, slot, j:j + 1], before[:, :],
                                           ALU.is_equal, ALU.mult, accum_out=dup[:, r, j:j + 1]).then_inc(S.R_dup, 1)
                    ins = v.tensor_scalar(SAME[:, r, j, :], row_j, s_col[:, slot, j:j + 1], w_col[:, slot, j:j + 1],
                                          ALU.is_equal, ALU.mult)
                ins.then_inc(S.R_same, 1)
                v.tensor_scalar(far[:, r, :], s_col[:, slot, :], -1.0, trash[:, :], ALU.mult, ALU.add)\
                    .then_inc(S.R_far, 1)

            def r_moved(q, r):
                dve.wait_ge(S.R_dup, GR * (q + 1) if isinstance(q, int) else GR * q + GR)
                dve.wait_ge(S.R_far, q + 1)
                v.scalar_tensor_tensor(moved[:, r, :], dup[:, r, :], 0.0, far[:, r, :], ALU.is_gt, ALU.mult)\
                    .then_inc(S.R_moved, 1)

            def r_idx(q, r, slot):
                dve.wait_ge(S.R_moved, q + 1)
                for j in range(GR):
                    wait(dve, scattered[j], 0 if isinstance(q, int) and q < 4 else 16 * (q - 3))
                v.tensor_tensor(s_idx[:, slot, :], moved[:, r, :], s_col[:, slot, :], ALU.add).then_inc(S.R_idx, 1)

            def r_body(i, first, t, last):
                for g in range(UG):
                    q = first + g
                    if not last or g + 2 < UG:
                        r_onehots(q + 2, (g + 2) % 4)
                    r_moved(q, g % 2)
                    if not last or g + 1 < UG:
                        r_same(q + 1, (g + 1) % 2, (g + 1) % 4)
                    r_idx(q, g % 2, g)
            r_onehots(0, 0)
            r_onehots(1, 1)
            r_same(0, 0, 0)
            over_pairs(dve, r_body)
            for h, loaded in enumerate((S.acc_loaded0, S.acc_loaded1)):
                dve.wait_ge(loaded, 16 * 2 * GR)
                total = half(A, h)[0:PB, :]
                link(v.tensor_tensor(total, total, half(A, h, A2)[0:PB, :], ALU.add))
                link(v.tensor_tensor(total, total, half(HR, h)[0:PB, :], ALU.add))
                dve.wait_ge(S.S_sum, h + 1)
                link(v.tensor_tensor(total, total, half(HR, h, H2)[0:PB, :], ALU.add))
                for b in range(h * (NB // 2), (h + 1) * (NB // 2)):
                    v.bn_stats(stat(b), node(A, b, D)).then_inc(S.S_stat, 1)
            phase_ended(dve, "S")
            norm(2 * L + 1, D)

            def e_q(b, r):
                dve.wait_ge(S.E_ps, b + 1)
                v.tensor_tensor(node(HR, b, D), PS[0:PB, 6 + r, 0:D], r_eb[0:PB, :], ALU.add).then_inc(S.E_q, 1)

            def e_init(b, r):
                dve.wait_ge(S.E_x, b + 1)
                v.tensor_scalar(node(HR, b, D, H2), zs[0:PB, r, 0:D], onepe[0:PB, :], None, ALU.mult)\
                    .then_inc(S.E_init, 1)
            over_blocks(dve, [(4, e_q), (1, e_init)])
            phase_ended(dve, "E")
            sums(L)
            over_blocks(dve, biased(6, S.F_ops, 0, None, D, S.F_v, S.F_stat, A, 0, X, 4))
            phase_ended(dve, "F")
            norm(2 * L + 2, D)

            def g_res(b, r):
                v.tensor_scalar(node(X, b, D), node(A, b, D), column(rstd, b), column(nmr, b), ALU.mult, ALU.add)\
                    .then_inc(S.G_res, 1)
            over_blocks(dve, [(0, normed(A, D, 0, [S.G_tr], S.G_x)), (0, g_res)])
            phase_ended(dve, "G")
            sums(L + 1)

            for c in range(NCH + 3):
                if c < NCH:
                    v.tensor_tensor(chunk(HR, c, D), chunk(A, c, D, A2), per_node(dinv, c, D), ALU.mult)\
                        .then_inc(S.H_o, 1)
                if 1 <= c <= NCH:
                    k = c - 1
                    dve.wait_ge(S.H_b, k + 1)
                    v.tensor_scalar(chunk(HR, k, D, H2), chunk(HR, k, D), 0.0, c_a[0:PB, :], ALU.min, ALU.mult)\
                        .then_inc(S.H_n, 1)
                    dve.wait_ge(S.H_n, k + 1)
                    v.scalar_tensor_tensor(chunk(HR, k, D), chunk(HR, k, D), 0.0, chunk(HR, k, D, H2), ALU.max,
                                           ALU.add).then_inc(S.H_p, 1)
                if c >= 3:
                    dve.wait_ge(S.H_v, c - 2)
                    for b in range((c - 3) * BC, (c - 2) * BC):
                        v.bn_stats(stat(b), node(A, b, D)).then_inc(S.H_stat, 1)
            phase_ended(dve, "H")
            norm(2 * L + 3, D)
            for c in range(NCH):
                v.tensor_tensor(chunk(HR, c, D), chunk(A, c, D), per_node(ln[:, 6, :], c, D), ALU.mult)\
                    .then_inc(S.I_m, 1)


_INS = ["x", "src", "dst", "edge_weight", "L0_gnn_t", "L0_gnn_time_w1", "L0_gnn_time_b1", "L0_gnn_time_w2",
        "L0_gnn_time_b2", "L0_gnn_in_w", "L0_gnn_in_b", "L0_gnn_gcn_w", "L0_gnn_gcn_b", "L0_gnn_res_w1",
        "L0_gnn_res_b1", "L0_gnn_res_g1", "L0_gnn_res_be1", "L0_gnn_res_w2", "L0_gnn_res_b2", "L0_gnn_res_g2",
        "L0_gnn_res_be2", "L0_gnn_out_w1", "L0_gnn_out_b1", "L0_gnn_out_w2", "L0_gnn_out_b2", "L1_gnn_W", "L1_gnn_b",
        "L2_gnn_W_edge", "L2_gnn_b_edge", "L2_gnn_W1", "L2_gnn_b1", "L2_gnn_W2", "L2_gnn_b2", "L2_gnn_eps",
        "L3_gnn_W", "L3_gnn_b", "L3_gnn_a"]


def kernel(**inputs):
    import numpy as np
    import concourse.bacc as bacc
    from concourse.bass_utils import run_bass_kernel_spmd as run

    nc = bacc.Bacc("TRN2", target_bir_lowering=False, num_devices=1)
    arrays, args = {}, {}
    for name in _INS:
        v = np.ascontiguousarray(inputs[name])
        if v.ndim == 0:
            v = v.reshape(1)
        arrays[f"in_{name}"] = v
        args[name] = nc.dram_tensor(f"in_{name}", v.shape, mybir.dt.from_np(v.dtype), kind="ExternalInput").ap()
    out = nc.dram_tensor("out_0", (N, D), f32, kind="ExternalOutput").ap()
    gnn(nc, namedtuple("Inputs", _INS)(**args), out)
    r = run(nc, [arrays], core_ids=[0])
    return r.results[0]["out_0"]
```
